# Optimizing a Trainium2 kernel written in Bass

```python
import numpy as np
import jax
import jax.numpy as jnp

def _softmax(x, axis=-1):
    return jax.nn.softmax(x, axis=axis)

def _gelu(x):
    return jax.nn.gelu(x, approximate=True)

def _silu(x):
    return jax.nn.silu(x)

def _sigmoid(x):
    return jax.nn.sigmoid(x)

def _layernorm(x, axis=-1, eps=1e-05):
    m = jnp.mean(x, axis=axis, keepdims=True)
    v = jnp.var(x, axis=axis, keepdims=True)
    return (x - m) / jnp.sqrt(v + eps)

def _scatter_add(tgt, idx, src, axis=0):
    return tgt.at[idx].add(src)

def _segment_sum(src, seg, n):
    return jax.ops.segment_sum(src, seg, n)
kernel_name = 'mk_xattn_ffn_d2_seqx_r8_19baac'

def setup_inputs(seed: int=0):
    np.random.seed(seed)
    _w = jnp.asarray

    def _rec_inputs():
        import jax
        import jax.numpy as jnp
        _rk = jax.random.key(seed)
        x = 7.22e-05 + 1 * jax.random.normal(jax.random.fold_in(_rk, 1), (4, 512, 128), jnp.float32)
        _lenS = 512 - jax.random.randint(jax.random.fold_in(_rk, 7), (4,), 0, max(1, 512 // 4) + 1, jnp.int32)
        _lenS2 = 77 - jax.random.randint(jax.random.fold_in(_rk, 8), (4,), 0, max(1, 77 // 4) + 1, jnp.int32)
        _ctx_768P = jax.random.normal(jax.random.fold_in(_rk, 11), (4, 16, 96), jnp.float32)
        _ctx_768c = jax.random.dirichlet(jax.random.fold_in(_rk, 511), 0.3 * jnp.ones((16,), jnp.float32), (4, 77))
        _ctx_768t = jnp.einsum('bsk,bkd->bsd', _ctx_768c, _ctx_768P)
        _ctx_768t = _ctx_768t * jax.lax.rsqrt(jnp.mean(jnp.square(_ctx_768t)) + 1e-12) * 0.953939
        ctx_768 = -0.000191848 + 0.999787 * (_ctx_768t + 0.3 * jax.random.normal(jax.random.fold_in(_rk, 611), (4, 77, 96), jnp.float32))
        _validS = jnp.arange(512)[None, :] < _lenS[:, None]
        _validS2 = jnp.arange(77)[None, :] < _lenS2[:, None]
        _causal = jnp.tril(jnp.ones((512, 512), dtype=bool))
        mask_BxS2_bf1 = jnp.ones((4, 77), dtype=bool)
        return (x, ctx_768, mask_BxS2_bf1)
    x, ctx_768, mask_BxS2_bf1 = _rec_inputs()

    def _L0_xattn_setup():
        import jax, jax.numpy as jnp
        import numpy as np
        N_HEADS = 16
        key = jax.random.key(seed)
        ks = jax.random.split(key, 8)
        b, l, m = (8, 128, 128)
        d_embed, d_cross = (128, 96)
        s_q = 1.0 / np.sqrt(d_embed)
        s_kv = 1.0 / np.sqrt(d_cross)
        return {'x': jax.random.normal(ks[0], (b, l, d_embed), jnp.float32), 'y': jax.random.normal(ks[1], (b, m, d_cross), jnp.float32), 'Wq': jax.random.normal(ks[2], (d_embed, d_embed), jnp.float32) * s_q, 'bq': jax.random.normal(ks[3], (d_embed,), jnp.float32) * 0.01, 'Wkv': jax.random.normal(ks[4], (2 * d_embed, d_cross), jnp.float32) * s_kv, 'bkv': jax.random.normal(ks[5], (2 * d_embed,), jnp.float32) * 0.01, 'Wo': jax.random.normal(ks[6], (d_embed, d_embed), jnp.float32) * s_q, 'bo': jax.random.normal(ks[7], (d_embed,), jnp.float32) * 0.01}
    _L0_xattn_all = _L0_xattn_setup()
    _L0_xattn_in = {k: v for k, v in _L0_xattn_all.items() if k in ('Wq', 'bq', 'Wkv', 'bkv', 'Wo', 'bo')}
    del _L0_xattn_all

    def _L0_ffn_setup():
        import jax, jax.numpy as jnp
        import numpy as np
        QMAX = 127.0

        def _ste_round(v):
            return v + jax.lax.stop_gradient(jnp.round(v) - v)

        def _act_fake_quant(x, clip_factor):
            scale = jax.nn.sigmoid(clip_factor) * jnp.max(jnp.abs(x)) / QMAX
            return jnp.clip(_ste_round(x / scale), -QMAX - 1.0, QMAX) * scale

        def _weight_fake_quant(w):
            scale = jnp.max(jnp.abs(w), axis=1, keepdims=True) / QMAX
            return jnp.clip(_ste_round(w / scale), -QMAX - 1.0, QMAX) * scale
        key = jax.random.key(seed)
        k1, k2, k3, k4 = jax.random.split(key, 4)
        B, S, H, I = (8, 1024, 128, 352)
        return {'x': jax.random.normal(k1, (B, S, H), dtype=jnp.float32), 'clip_x': jnp.full((1,), 4.0, dtype=jnp.float32), 'clip_down': jnp.full((1,), 4.0, dtype=jnp.float32), 'w_gate': jax.random.normal(k2, (I, H), dtype=jnp.float32) * 0.02, 'w_up': jax.random.normal(k3, (I, H), dtype=jnp.float32) * 0.02, 'w_down': jax.random.normal(k4, (H, I), dtype=jnp.float32) * 0.02}
    _L0_ffn_all = _L0_ffn_setup()
    _L0_ffn_in = {k: v for k, v in _L0_ffn_all.items() if k in ('clip_x', 'clip_down', 'w_gate', 'w_up', 'w_down')}
    del _L0_ffn_all

    def _L1_xattn_setup():
        import jax, jax.numpy as jnp
        import numpy as np
        DIM = 128
        CTX_DIM = 96
        HEADS = 16
        key = jax.random.key(seed)
        ks = jax.random.split(key, 7)
        B, N, M = (4, 512, 32)
        x = jax.random.normal(ks[0], (B, N, DIM), dtype=jnp.float32)
        context = jax.random.normal(ks[1], (B, M, CTX_DIM), dtype=jnp.float32)
        context_mask = jnp.ones((B, M), dtype=bool)
        s_d = 1.0 / np.sqrt(DIM)
        s_c = 1.0 / np.sqrt(CTX_DIM)
        Wq = jax.random.normal(ks[2], (DIM, DIM), dtype=jnp.float32) * s_d
        Wk = jax.random.normal(ks[3], (CTX_DIM, DIM), dtype=jnp.float32) * s_c
        Wv = jax.random.normal(ks[4], (CTX_DIM, DIM), dtype=jnp.float32) * s_c
        Wo = jax.random.normal(ks[5], (DIM, DIM), dtype=jnp.float32) * s_d
        return {'x': x, 'context': context, 'context_mask': context_mask, 'Wq': Wq, 'Wk': Wk, 'Wv': Wv, 'Wo': Wo}
    _L1_xattn_all = _L1_xattn_setup()
    _L1_xattn_in = {k: v for k, v in _L1_xattn_all.items() if k in ('Wq', 'Wk', 'Wv', 'Wo')}
    del _L1_xattn_all

    def _L1_ffn_setup():
        import jax, jax.numpy as jnp
        import numpy as np
        TEMPERATURE = 0.5
        CAPACITY_FACTOR = 1.25
        TOP_K = 1
        key = jax.random.key(seed)
        ks = jax.random.split(key, 5)
        B, S, D, H, E = (4, 256, 128, 256, 8)
        s = 0.02
        return {'x': jax.random.normal(ks[0], (B, S, D), jnp.float32), 'gate_w': jax.random.normal(ks[1], (E, D), jnp.float32) * s, 'gate_b': jnp.zeros((E,), jnp.float32), 'rms_w': jnp.ones((E,), jnp.float32), 'w1': jax.random.normal(ks[2], (E, D, H), jnp.float32) * s, 'b1': jnp.zeros((E, H), jnp.float32), 'w2': jax.random.normal(ks[3], (E, H, D), jnp.float32) * s, 'b2': jnp.zeros((E, D), jnp.float32)}
    _L1_ffn_all = _L1_ffn_setup()
    _L1_ffn_in = {k: v for k, v in _L1_ffn_all.items() if k in ('gate_w', 'gate_b', 'rms_w', 'w1', 'b1', 'w2', 'b2')}
    del _L1_ffn_all
    return {'x': x, 'ctx_768': ctx_768, 'mask_BxS2_bf1': mask_BxS2_bf1, 'L0_xattn_Wq': _L0_xattn_in['Wq'], 'L0_xattn_bq': _L0_xattn_in['bq'], 'L0_xattn_Wkv': _L0_xattn_in['Wkv'], 'L0_xattn_bkv': _L0_xattn_in['bkv'], 'L0_xattn_Wo': _L0_xattn_in['Wo'], 'L0_xattn_bo': _L0_xattn_in['bo'], 'L0_ffn_clip_x': _L0_ffn_in['clip_x'], 'L0_ffn_clip_down': _L0_ffn_in['clip_down'], 'L0_ffn_w_gate': _L0_ffn_in['w_gate'], 'L0_ffn_w_up': _L0_ffn_in['w_up'], 'L0_ffn_w_down': _L0_ffn_in['w_down'], 'L1_xattn_Wq': _L1_xattn_in['Wq'], 'L1_xattn_Wk': _L1_xattn_in['Wk'], 'L1_xattn_Wv': _L1_xattn_in['Wv'], 'L1_xattn_Wo': _L1_xattn_in['Wo'], 'L1_ffn_gate_w': _L1_ffn_in['gate_w'], 'L1_ffn_gate_b': _L1_ffn_in['gate_b'], 'L1_ffn_rms_w': _L1_ffn_in['rms_w'], 'L1_ffn_w1': _L1_ffn_in['w1'], 'L1_ffn_b1': _L1_ffn_in['b1'], 'L1_ffn_w2': _L1_ffn_in['w2'], 'L1_ffn_b2': _L1_ffn_in['b2']}

def reference(x, ctx_768, mask_BxS2_bf1, L0_xattn_Wq, L0_xattn_bq, L0_xattn_Wkv, L0_xattn_bkv, L0_xattn_Wo, L0_xattn_bo, L0_ffn_clip_x, L0_ffn_clip_down, L0_ffn_w_gate, L0_ffn_w_up, L0_ffn_w_down, L1_xattn_Wq, L1_xattn_Wk, L1_xattn_Wv, L1_xattn_Wo, L1_ffn_gate_w, L1_ffn_gate_b, L1_ffn_rms_w, L1_ffn_w1, L1_ffn_b1, L1_ffn_w2, L1_ffn_b2):
    import jax
    import jax.numpy as jnp

    def _L0_xattn_ref(x, y, Wq, bq, Wkv, bkv, Wo, bo):
        import jax, jax.numpy as jnp
        import numpy as np
        N_HEADS = 16
        b, l, d = x.shape
        m = y.shape[1]
        h = N_HEADS
        dh = d // h
        q = (jnp.einsum('bld,ed->ble', x, Wq) + bq).reshape(b, l, h, dh)
        kv = (jnp.einsum('bmc,ec->bme', y, Wkv) + bkv).reshape(b, m, h, 2 * dh)
        k, v = (kv[..., :dh], kv[..., dh:])
        scale = 1.0 / jnp.sqrt(jnp.asarray(dh, x.dtype))
        att = jax.nn.softmax(jnp.einsum('blhd,bmhd->blmh', q, k) * scale, axis=2)
        out = jnp.einsum('blmh,bmhd->blhd', att, v).reshape(b, l, d)
        return jnp.einsum('bld,ed->ble', out, Wo) + bo

    def _L0_ffn_ref(x, clip_x, clip_down, w_gate, w_up, w_down):
        import jax, jax.numpy as jnp
        import numpy as np
        QMAX = 127.0

        def _ste_round(v):
            return v + jax.lax.stop_gradient(jnp.round(v) - v)

        def _act_fake_quant(x, clip_factor):
            scale = jax.nn.sigmoid(clip_factor) * jnp.max(jnp.abs(x)) / QMAX
            return jnp.clip(_ste_round(x / scale), -QMAX - 1.0, QMAX) * scale

        def _weight_fake_quant(w):
            scale = jnp.max(jnp.abs(w), axis=1, keepdims=True) / QMAX
            return jnp.clip(_ste_round(w / scale), -QMAX - 1.0, QMAX) * scale
        xq = _act_fake_quant(x, clip_x[0])
        gate = jnp.einsum('bsh,ih->bsi', xq, _weight_fake_quant(w_gate))
        up = jnp.einsum('bsh,ih->bsi', xq, _weight_fake_quant(w_up))
        h = _act_fake_quant(jax.nn.silu(gate) * up, clip_down[0])
        return jnp.einsum('bsi,hi->bsh', h, _weight_fake_quant(w_down))

    def _L1_xattn_ref(x, context, context_mask, Wq, Wk, Wv, Wo):
        import jax, jax.numpy as jnp
        import numpy as np
        DIM = 128
        CTX_DIM = 96
        HEADS = 16
        B, N, _ = x.shape
        M = context.shape[1]
        hd = DIM // HEADS
        scale = hd ** (-0.5)
        q = (x @ Wq).reshape(B, N, HEADS, hd).transpose(0, 2, 1, 3)
        k = (context @ Wk).reshape(B, M, HEADS, hd).transpose(0, 2, 1, 3)
        v = (context @ Wv).reshape(B, M, HEADS, hd).transpose(0, 2, 1, 3)
        scores = jnp.einsum('bhid,bhjd->bhij', q, k) * scale
        max_neg = -jnp.finfo(scores.dtype).max
        scores = jnp.where(context_mask[:, None, None, :], scores, max_neg)
        attn = jax.nn.softmax(scores, axis=-1)
        out = jnp.einsum('bhij,bhjd->bhid', attn, v)
        out = out.transpose(0, 2, 1, 3).reshape(B, N, DIM)
        return out @ Wo

    def _L1_ffn_ref(x, gate_w, gate_b, rms_w, w1, b1, w2, b2):
        import jax, jax.numpy as jnp
        import numpy as np
        TEMPERATURE = 0.5
        CAPACITY_FACTOR = 1.25
        TOP_K = 1
        B, S, D = x.shape
        E = gate_w.shape[0]
        xf = x.reshape(-1, D)
        N = xf.shape[0]
        logits = xf @ gate_w.T + gate_b
        eps = jnp.finfo(logits.dtype).eps
        ms = jnp.mean(logits * logits, axis=-1, keepdims=True)
        logits = logits * jax.lax.rsqrt(ms + eps) * rms_w
        gates = jax.nn.softmax(logits / TEMPERATURE, axis=-1)
        g, idx = jax.lax.top_k(gates, TOP_K)
        g, idx = (g[:, 0], idx[:, 0])
        capacity = min(int(np.ceil(N * TOP_K / E * CAPACITY_FACTOR)), N)
        counts = jnp.zeros((E,), jnp.int32).at[idx].add(1)
        active = (counts > 0) & (capacity >= 1)
        mask = active[idx].astype(gates.dtype)
        masked = g * mask
        norm_g = masked / (masked + 1e-06)
        h = jax.nn.gelu(jnp.einsum('nd,edh->neh', xf, w1) + b1, approximate=False)
        y = jnp.einsum('neh,ehd->ned', h, w2) + b2
        out = (y * norm_g[:, None, None]).sum(axis=1)
        return out.reshape(B, S, D)
    x = x + _L0_xattn_ref(_layernorm(x, axis=-1), ctx_768, L0_xattn_Wq, L0_xattn_bq, L0_xattn_Wkv, L0_xattn_bkv, L0_xattn_Wo, L0_xattn_bo)
    x = x + _L0_ffn_ref(_layernorm(x, axis=-1), L0_ffn_clip_x, L0_ffn_clip_down, L0_ffn_w_gate, L0_ffn_w_up, L0_ffn_w_down)
    x = x + _L1_xattn_ref(_layernorm(x, axis=-1), ctx_768, mask_BxS2_bf1, L1_xattn_Wq, L1_xattn_Wk, L1_xattn_Wv, L1_xattn_Wo)
    x = x + _L1_ffn_ref(_layernorm(x, axis=-1), L1_ffn_gate_w, L1_ffn_gate_b, L1_ffn_rms_w, L1_ffn_w1, L1_ffn_b1, L1_ffn_w2, L1_ffn_b2)
    return x

_drawn_inputs = setup_inputs


def setup_inputs(seed=0):
    import zlib

    import numpy as np

    out = dict(_drawn_inputs(seed))
    spreads = {'L1_ffn_gate_b': (0.0, 2.0),
     'L1_ffn_rms_w': (1.0, 0.6),
     'L1_ffn_b1': (0.0, 0.762),
     'L1_ffn_b2': (0.0, 0.1)}
    factors = {'L0_xattn_bq': 8.0,
     'L0_xattn_bkv': 6.433,
     'L0_xattn_bo': 6.84,
     'L0_ffn_w_gate': 7.261,
     'L0_ffn_w_up': 6.948,
     'L0_ffn_w_down': 6.961,
     'L1_ffn_gate_w': 64.0}
    for name, (base, spread) in spreads.items():
        noise = np.random.default_rng([zlib.crc32(name.encode()), seed]).standard_normal(out[name].shape)
        drawn = base * np.exp(spread * noise) if base else spread * noise
        out[name] = jnp.asarray(drawn.astype(out[name].dtype))
    for name, factor in factors.items():
        out[name] = (out[name] * factor).astype(out[name].dtype)
    return out
```

```python
from contextlib import ExitStack

import numpy as np

import concourse.bass as bass
from concourse import mybir

F32 = mybir.dt.float32
F32R = mybir.dt.float32r
BF16 = mybir.dt.bfloat16
U8 = mybir.dt.uint8
ALU = mybir.AluOpType
ACT = mybir.ActivationFunctionType
AX = mybir.AxisListType

B, S, D = 4, 512, 128
NT = S // 128
M, MP = 77, 78
C = 96
H, HD = 16, 8
G, HG = 4, 4
NC = 3
JC = MP // NC
PR = JC * HG
KG = MP * HG
VW = HD + 1
MASKROW, MHI, MLO, KROWS = 96, 97, 101, 105
I0 = 352
IT = [128, 128, 96]
E, HE = 8, 256
NH = E * HE // 128
STQ, STM = 16 * 3 * G, 16 * 2 * G
SCALE = float(HD) ** -0.5
NEG = -(2.0 ** 127)
MAGIC = 1.5 * 2.0 ** 23
QMAX = 127.0
LN_EPS = 1e-5
EPS32 = float(np.finfo(np.float32).eps)
STOP = 9


def build(nc, a, out):
    with ExitStack() as ctx:
        def sb(name, shape, dt=F32):
            return ctx.enter_context(nc.sbuf_tensor(name, shape, dt))

        def ps(name):
            return ctx.enter_context(nc.psum_tensor(name, [128, 512], F32))

        def sem(name):
            return ctx.enter_context(nc.semaphore(name))

        x = sb("x", [128, B * NT, D])
        xn = sb("xn", [128, B * NT, D])
        stats = sb("stats", [128, B, NT, 6])
        mv = sb("mv", [128, B, NT, 2])
        veps = sb("veps", [128, B, NT])
        rstd = sb("rstd", [128, B, NT])
        mhalf = sb("mhalf", [128, NT * E])
        ebase = sb("ebase", [128, NT * E])
        ident = sb("ident_sb", [128, 128])
        magic = sb("magic", [128, 1])
        ctxt = sb("ctxt", [C + 1, B * MP])
        wk = sb("wk", [C + 1, 2, D])
        wv = sb("wv", [C + 1, 2, D])
        wq = sb("wq", [D, 2, D])
        wo = sb("wo", [D, 2, D])
        bq = sb("bq", [D, 2])
        bo = sb("bo_sb", [128, D])
        kmask = sb("kmask_sb", [128, HG])
        vmask = sb("vmask_sb", [PR, H])
        cmask = sb("cmask", [128, B, MP], U8)
        khi = sb("khi", [D, B * MP], F32R)
        klo = sb("klo", [D, B * MP], F32R)
        rbuf = sb("rbuf", [128, 6 * S], F32R)
        kbd = rbuf[:, 0:2 * B * KG].rearrange("p (s c h) -> p s c h", s=2, h=HG)
        hh = rbuf[:, 0:3 * S].rearrange("p (n c) -> p n c", n=3)
        hl = rbuf[:, 3 * S:6 * S].rearrange("p (n c) -> p n c", n=3)
        kextra = sb("kextra", [128, B * KG])
        kst = sb("kst", [128, B, G, KG], F32R)
        vbd = sb("vbd", [PR, 2, B, NC, H * VW])
        qhi = sb("qhi", [128, 2, S], F32R)
        qlo = sb("qlo", [128, 2, S], F32R)
        qst = sb("qst", [128, 2, G, S], F32R)
        mx = sb("mx", [128, 2, NT, H])
        mthi = sb("mthi", [H, 2, S], F32R)
        mtlo = sb("mtlo", [H, 2, S], F32R)
        big = sb("big", [128, G * NC * S])
        p = big[0:PR, :].rearrange("p (n c) -> p n c", n=G * NC)
        h0 = big[:, :].rearrange("p (b n c) -> p b n c", b=B, n=3)
        hf = big[:, 0:3 * S].rearrange("p (n c) -> p n c", n=3)
        yt = big[:, 3 * S:4 * S]
        ctxr = big[0:C + 1, 0:B * KG].rearrange("p (j h) -> p j h", h=HG)
        kf = big[:, B * KG:B * KG + B * MP]
        tbuf = sb("tbuf", [128, 6 * S])
        xt = tbuf[:, 0:2 * S].rearrange("p (n c) -> p n c", n=2)
        ot = tbuf[:, 2 * S:4 * S].rearrange("p (n c) -> p n c", n=2)
        on = tbuf[:, 4 * S:6 * S].rearrange("p (s t d) -> p s t d", s=2, t=NT)
        hq = tbuf[:, :].bitcast(BF16).rearrange("p (b n c) -> p b n c", b=B, n=3)
        sbuf4 = sb("sbuf4", [128, 2 * S])
        sg = sbuf4[:, :].rearrange("p (n c) -> p n c", n=2)
        dtmp = sbuf4[:, :].rearrange("p (n c) -> p n c", n=2)
        rden = sb("rden", [128, 2, H])

        wg0 = sb("wg0", [128, 3, D])
        wu0 = sb("wu0", [128, 3, D])
        wd0 = sb("wd0", [D, I0])
        wmx = sb("wmx", [128, 7])
        rwm = sb("rwm", [128, 7])
        wgT = sb("wgT", [D, I0], BF16)
        wuT = sb("wuT", [D, I0], BF16)
        wdT = sb("wdT", [128, 3, D], BF16)
        clip = sb("clip", [128, 2])
        eclip = sb("eclip", [128, 2])
        csc = sb("csc", [128, 2])
        diag = sb("diag", [D, D])
        sdrow = sb("sdrow", [128, D])
        ones = sb("ones", [128, 128])
        axb = sb("axb", [128, 2, B])
        axm = sb("axm", [128, 2])
        gm1 = sb("gm1", [1, 2])
        qs = sb("qs", [128, 2])
        rqs = sb("rqs", [128, 2])
        gus = sb("gus", [128, 6])
        xqt = sb("xqt", [D, B, S], BF16)

        w1f = sb("w1f", [128, E * HE])
        w1h = sb("w1h", [128, E * HE], F32R)
        w1l = sb("w1l", [128, E * HE], F32R)
        w2h = sb("w2h", [128, NH * D], F32R)
        w2l = sb("w2l", [128, NH * D], F32R)
        b1 = sb("b1", [128, NH])
        b2 = sb("b2", [D, E])
        b2s = sb("b2s", [D, 1])
        gwf = sb("gwf", [D, E])
        gwh = sb("gwh", [D, E], F32R)
        gwl = sb("gwl", [D, E], F32R)
        gb = sb("gb", [128, E])
        rw = sb("rw", [128, E])
        xh1, xl1 = qhi, qlo
        lg = sb("lg", [128, NT, E])
        lq = sb("lq", [128, NT, E])
        s4 = sb("s4", [128, 6, NT])
        ng = sb("ng", [128, 2, NT])

        tok = [ps(f"ps_tok{i}") for i in range(2)]
        key = [ps(f"ps_key{i}") for i in range(2)]
        acc = [ps(f"ps_acc{i}") for i in range(2)]
        m0 = ps("ps_m0")
        m1 = ps("ps_m1")

        x_in = [sem(f"x_in{b}") for b in range(B)]
        s_names = (
            "consts_in bo_in ctx_in watt_in mask_in wffn_in clip_in w1_in w2_in gate_in "
            "const_set wf_ready extra_ready ctxr_ready kt_put k_split kst_in krow_set vr_put v_set xb_set "
            "var_ready eps_self rstd_ready xn_ready xt_put xt_copied q_put q_hi q_lo "
            "tok_put tok_maxed mt_put mt_hi mt_lo key_put p_ready o_put o_normed ot_put ot_copied "
            "att_put x_attended dve_self act_self pool_self "
            "wq_rounded wqT_put wqT_copied sd_diag sd_put sd_copied csc_ready "
            "part_max row_put row_max bc_put xq_ready xqt_put xqt_copied g_put u_put silu_ready h_ready "
            "hq_f hq_ready d_put x_ffn w1_split w1_free w2_split b2_summed xt1_put x1_hi x1_lo lg_put lg_ms lg_r lg_d lg_e "
            "ng_ready w1_put gelu_ready h_split w2_done yt_copied yT_put y_done out_done"
        )
        q = {n: sem(n) for n in s_names.split()}
        stack_q = [sem(f"stack_q{i}") for i in range(2)]
        stack_m = [sem(f"stack_m{i}") for i in range(2)]

        block = ctx.enter_context(nc.Block())
        UNITS = range(B)
        AT_XT, AT_Q, AT_OT, AT_WO, AT_LN, LAG, LAGV = 2, 5, 9, 11, 14, 4, 8

        def pv_turn(i, k):
            return (i, *divmod(k - LAGV, NT)) if k >= LAGV else (i - 1, *divmod(k + 16 - LAGV, NT))

        def steps(first_step, last_step):
            for i in range(first_step, last_step + 1):
                for k in range(16):
                    yield i, k

        @block.sync
        def _(sp):
            for b in range(B):
                sp.dma_start(x[:, NT * b:NT * b + NT, :], a["x"][b].rearrange("(t p) d -> p t d", p=128)).then_inc(x_in[b], 16)
                if b == 0:
                    sp.dma_start(ident[:, :], a["ident"]).then_inc(q["consts_in"], 16)
                    sp.dma_start(kmask[:, :], a["kmask"]).then_inc(q["consts_in"], 16)
                    sp.dma_start(vmask[:, :], a["vmask"]).then_inc(q["consts_in"], 16)
            sp.dma_start(bo[:, :], a["bo"].partition_broadcast(128)).then_inc(q["bo_in"], 16)
            sp.dma_start(clip[:, :], a["clip"].partition_broadcast(128)).then_inc(q["clip_in"], 16)
            for w, src in ((wg0, a["w_gate"]), (wu0, a["w_up"])):
                sp.dma_start(w[:, 0:2, :], src[0:256, :].rearrange("(t p) d -> p t d", p=128)).then_inc(q["wffn_in"], 16)
                sp.dma_start(w[0:IT[2], 2, :], src[256:I0, :]).then_inc(q["wffn_in"], 16)
            sp.dma_start(wd0[:, :], a["w_down"]).then_inc(q["wffn_in"], 16)

            def stack(dst, src, rows, done):
                for g in range(G):
                    sp.dma_start(dst[:, g, :].bitcast(F32), src[rows * g:rows * g + rows, :].bitcast(F32)).then_inc(done, 16)

            for L in range(2):
                sp.wait_ge(q["k_split"], L + 1)
                if L == 1:
                    sp.wait_ge(q["key_put"], 12 * B)
                for g in range(G):
                    for r, half in enumerate((0, 0, 1)):
                        sp.dma_start(kst[32 * r:32 * r + 32, :, g, :].bitcast(F32),
                                     kbd[32 * g:32 * g + 32, half, :, :].rearrange("p (b j) h -> p b (j h)", b=B).bitcast(F32)
                                     ).then_inc(q["kst_in"], 16)
                for i in range(-2, B):
                    if i + 2 < B:
                        u = B * L + i + 2
                        s = u % 2
                        sp.wait_ge(q["q_hi"], u + 1)
                        if u >= 2:
                            sp.wait_ge(q["key_put"], 12 * (u - 1))
                        for r in (0, 2):
                            stack(qst[32 * r:32 * r + 32, s], qhi[:, s, :], 32, stack_q[s])
                        sp.wait_ge(q["q_lo"], u + 1)
                        stack(qst[32:64, s], qlo[:, s, :], 32, stack_q[s])
                    if 0 <= i + 1 < B:
                        u = B * L + i + 1
                        s = u % 2
                        sp.wait_ge(q["mt_hi"], u + 1)
                        stack(qst[MHI:MHI + HG, s], mthi[:, s, :], HG, stack_m[s])
                        sp.wait_ge(q["mt_lo"], u + 1)
                        stack(qst[MLO:MLO + HG, s], mtlo[:, s, :], HG, stack_m[s])
            for b in range(B):
                sp.wait_ge(q["y_done"], b + 1)
                sp.dma_start(out[b].rearrange("(t p) d -> p t d", p=128), xn[:, NT * b:NT * b + NT, :]).then_inc(q["out_done"], 16)
            sp.wait_ge(q["out_done"], 16 * B)

        @block.gpsimd
        def _(pool):
            sent = {}

            def done(ins, name):
                sent[name] = sent.get(name, 0) + 1
                ins.then_inc(q[name], 1)
                pool.wait_ge(q[name], sent[name])

            for ap, value in ((mhalf[:, :], -0.5), (ebase[:, :], float(np.e)), (magic[:, :], -MAGIC), (ones[:, :], 1.0),
                              (qst[96:128, :, :, :].bitcast(F32), 1.0), (axb[:, :, :], 0.0)):
                done(nc.gpsimd.memset(ap, value), "pool_self")
            done(nc.gpsimd.memset(bq[:, 1:2], 0.0), "const_set")
            pool.dma_start(gwf[:, :], a["gate_wT"]).then_inc(q["gate_in"], 16)
            pool.dma_start(gb[:, :], a["gate_b"].partition_broadcast(128)).then_inc(q["gate_in"], 16)
            pool.dma_start(rw[:, :], a["rms_w"].partition_broadcast(128)).then_inc(q["gate_in"], 16)
            pool.dma_start(b1[:, :], a["b1"]).then_inc(q["gate_in"], 16)
            pool.dma_start(b2[:, :], a["b2"]).then_inc(q["gate_in"], 16)
            pool.dma_start(w1f[:, :].rearrange("d (e h) -> d e h", e=E), a["w1"].rearrange("e d h -> d e h")).then_inc(q["w1_in"], 16)

            def rstd_of(n):
                b = n % B
                pool.wait_ge(q["var_ready"], n + 1)
                done(nc.gpsimd.tensor_scalar(veps[:, b, :], mv[:, b, :, 1], LN_EPS, None, ALU.add), "eps_self")
                done(nc.gpsimd.tensor_tensor(rstd[:, b, :], veps[:, b, :], mhalf[:, 0:NT], ALU.pow), "rstd_ready")

            for b in range(B):
                rstd_of(b)
            pool.wait_ge(q["bo_in"], 16)
            for b in range(B):
                pool.wait_ge(q["xn_ready"], b + 1)
                for t in range(NT):
                    done(nc.gpsimd.tensor_tensor(x[:, NT * b + t, :], x[:, NT * b + t, :], bo[:, :], ALU.add), "xb_set")
            pool.wait_ge(q["w1_in"], 16)
            done(nc.gpsimd.tensor_copy(w1h[:, :], w1f[:, :]), "pool_self")
            done(nc.gpsimd.tensor_tensor(w1l[:, :], w1f[:, :], w1h[:, :].bitcast(F32), ALU.subtract), "w1_split")
            pool.dma_start(w1f[:, :].rearrange("p (n d) -> p n d", n=NH),
                           a["w2"].rearrange("e (s p) d -> p (e s) d", p=128)).then_inc(q["w2_in"], 16)
            pool.wait_ge(q["w2_in"], 16)
            done(nc.gpsimd.tensor_copy(w2h[:, :], w1f[:, :]), "pool_self")
            done(nc.gpsimd.tensor_tensor(w2l[:, :], w1f[:, :], w2h[:, :].bitcast(F32), ALU.subtract), "w2_split")
            for n in range(B, 3 * B if STOP > 2 else 2 * B if STOP < 2 else 3 * B):
                rstd_of(n)
            if STOP > 2:
                for n in range(3 * B, 4 * B):
                    rstd_of(n)
            if STOP > 3:
                for b in range(B):
                    pool.wait_ge(q["lg_ms"], b + 1)
                    done(nc.gpsimd.tensor_scalar(s4[:, 1, :], s4[:, 0, :], 1.0 / E, EPS32, ALU.mult, ALU.add), "pool_self")
                    done(nc.gpsimd.tensor_tensor(s4[:, 2, :], s4[:, 1, :], mhalf[:, 0:NT], ALU.pow), "lg_r")
                    pool.wait_ge(q["lg_d"], b + 1)
                    done(nc.gpsimd.tensor_tensor(lq[:, :, :], ebase[:, :].rearrange("p (t e) -> p t e", t=NT), lg[:, :, :], ALU.pow), "lg_e")

        @block.scalar
        def _(act):
            act.dma_start(ctxt[0:C, :].rearrange("c (b j) -> c b j", b=B), a["ctxT"]).then_inc(q["ctx_in"], 16)
            act.dma_start(ctxt[C:C + 1, :], a["ones_row"]).then_inc(q["ctx_in"], 16)
            act.dma_start(wk[:, :, :], a["wk"]).then_inc(q["watt_in"], 16)
            act.dma_start(wv[:, :, :], a["wv"]).then_inc(q["watt_in"], 16)
            act.dma_start(wq[:, :, :], a["wq"]).then_inc(q["watt_in"], 16)
            act.dma_start(wo[:, :, :], a["wo"]).then_inc(q["watt_in"], 16)
            act.dma_start(bq[:, 0:1], a["bq"]).then_inc(q["watt_in"], 16)
            act.dma_start(cmask[:, :, 0:M], a["mask"].partition_broadcast(128)).then_inc(q["mask_in"], 16)
            act.dma_start(kextra[96:KROWS, :], a["krows"]).then_inc(q["mask_in"], 16)

            act.wait_ge(q["ctx_in"], 32)
            act.activation(ctxr[:, :, :], ctxt[:, :].unsqueeze(2).broadcast_to([C + 1, B * MP, HG]), ACT.Copy).then_inc(q["ctxr_ready"], 1)
            act.wait_ge(q["mask_in"], 32)

            def key_rows(L):
                r = slice(96, KROWS)
                if L == 1:
                    act.wait_ge(q["extra_ready"], 1)
                    act.wait_ge(q["key_put"], 12 * B)
                for b in range(B):
                    src = kextra[r, b * KG:(b + 1) * KG]
                    act.activation(kst[r, b], src.unsqueeze(1).broadcast_to([KROWS - 96, G, KG]), ACT.Copy).then_inc(q["krow_set"], 1)

            key_rows(0)

            def quant_prep():
                act.wait_ge(q["clip_in"], 16)
                act.activation(eclip[:, :], clip[:, :], ACT.Exp, scale=-1.0).then_inc(q["csc_ready"], 1)
                act.wait_ge(q["const_set"], 1)
                for n, dst in enumerate((wgT, wuT)):
                    act.wait_ge(q["wqT_put"], n + 1)
                    act.activation(dst[:, :], tok[n][:, 0:I0], ACT.Identity, bias=magic[:, 0:1]).then_inc(q["wqT_copied"], 1)
                act.wait_ge(q["wqT_put"], 3)
                act.activation(wdT[:, 0:2, :], key[0][:, 0:256].rearrange("p (t d) -> p t d", t=2), ACT.Identity, bias=magic[:, 0:1]).then_inc(q["wqT_copied"], 1)
                act.activation(wdT[0:IT[2], 2, :], key[0][0:IT[2], 256:384], ACT.Identity, bias=magic[0:IT[2], 0:1]).then_inc(q["wqT_copied"], 1)

            def attention(L):
                for i, k in steps(-2, B):
                    e, n2, last, nxt = i, i + 2, i - 1, i + 1
                    u = B * L + i
                    if e in UNITS and k >= LAG:
                        n = 12 * u + k - LAG
                        act.wait_ge(q["key_put"], n + 1)
                        if u >= 1:
                            act.wait_ge(q["o_put"], G * (u - 1) + (k - LAG) // NC + 1)
                        act.activation(p[:, k - LAG, :], key[n % 2][0:PR, :], ACT.Exp, scale=SCALE).then_inc(q["p_ready"], 1)
                    if k == AT_OT and last in UNITS:
                        v = u - 1
                        act.wait_ge(q["ot_put"], v + 1)
                        if v >= 2:
                            act.wait_ge(q["att_put"], v - 1)
                        act.activation(ot[:, v % 2, :], m0[:, :], ACT.Copy).then_inc(q["ot_copied"], 1)
                    if k == AT_XT and n2 in UNITS:
                        v = u + 2
                        act.wait_ge(q["xt_put"], v + 1)
                        if v >= 2:
                            act.wait_ge(q["q_put"], v - 1)
                        act.activation(xt[:, v % 2, :], m0[:, :], ACT.Copy).then_inc(q["xt_copied"], 1)
                    if k == AT_Q and n2 in UNITS:
                        v = u + 2
                        act.wait_ge(q["q_put"], v + 1)
                        if v >= 2:
                            act.wait_ge(stack_q[v % 2], STQ * (v // 2))
                        if v == 0:
                            act.wait_ge(q["watt_in"], 80)
                            act.wait_ge(q["const_set"], 1)
                        act.activation(qhi[:, v % 2, :], m1[:, :], ACT.Identity, bias=bq[:, L:L + 1]).then_inc(q["q_hi"], 1)
                    if k == 15 and nxt in UNITS:
                        v = u + 1
                        act.wait_ge(q["mt_put"], v + 1)
                        if v >= 2:
                            act.wait_ge(stack_m[v % 2], STM * (v // 2))
                        act.activation(mthi[:, v % 2, :], m0[0:H, :], ACT.Copy).then_inc(q["mt_hi"], 1)
                    if L == 0 and i == -1 and k == 15:
                        quant_prep()

            attention(0)
            key_rows(1)
            if STOP > 1:
                for b in range(B):
                    act.wait_ge(q["xqt_put"], b + 1)
                    act.activation(xqt[:, b, :], (m0, m1)[b % 2][:, :], ACT.Identity, bias=magic[:, 0:1]).then_inc(q["xqt_copied"], 1)
                for n in range(3 * B):
                    b, i3 = divmod(n, 3)
                    w = IT[i3]
                    act.wait_ge(q["g_put"], n + 1)
                    if n >= 2:
                        act.wait_ge(q["h_ready"], n - 1)
                    act.activation(sg[0:w, n % 2, :], tok[n % 2][0:w, :], ACT.Silu, scale=gus[0:w, i3:i3 + 1]).then_inc(q["silu_ready"], 1)
                for b in range(B):
                    act.wait_ge(q["hq_f"], b + 1)
                    act.activation(hq[:, b, :, :], h0[:, b, :, :], ACT.Identity, bias=magic[:, 0:1]).then_inc(q["hq_ready"], 1)
            if STOP > 2:
                attention(1)
            if STOP > 3:
                def x_hi(b):
                    act.wait_ge(q["xt1_put"], b + 1)
                    if b >= 2:
                        act.wait_ge(q["w1_put"], NH * (b - 1))
                    act.activation(xh1[:, b % 2, :], m0[:, :], ACT.Copy).then_inc(q["x1_hi"], 1)

                x_hi(0)
                for n in range(NH * B + 4):
                    if n < NH * B:
                        act.wait_ge(q["w1_put"], n + 1)
                        if n >= 3:
                            act.wait_ge(q["h_split"], 2 * (n - 2))
                        act.activation(hf[:, n % 3, :], (tok + key)[n % 4][:, :], ACT.Gelu, bias=b1[:, n % NH:n % NH + 1]).then_inc(q["gelu_ready"], 1)
                    if n % NH == 8 and n // NH + 1 < B:
                        x_hi(n // NH + 1)
                    if n % NH == 3 and n >= NH:
                        b = n // NH - 1
                        act.wait_ge(q["w2_done"], NH * (b + 1))
                        if b == 0:
                            act.wait_ge(q["b2_summed"], 1)
                        if b >= 1:
                            act.wait_ge(q["yT_put"], b)
                        act.activation(yt[:, :], acc[b % 2][:, :], ACT.Identity, bias=b2s[:, 0:1]).then_inc(q["yt_copied"], 1)

        @block.vector
        def _(dve):
            link_n = [0]

            def link(ins):
                link_n[0] += 1
                ins.then_inc(q["dve_self"], 1)
                dve.wait_ge(q["dve_self"], link_n[0])

            def ln_stats(n):
                b = n % B
                for t in range(NT):
                    ins = nc.vector.bn_stats(stats[:, b, t, :], x[:, NT * b + t, :])
                link(ins)
                for t in range(NT):
                    ins = nc.vector.bn_aggr(mv[:, b, t, :], stats[:, b, t, :])
                ins.then_inc(q["var_ready"], 1)

            def ln_apply(n):
                b = n % B
                dve.wait_ge(q["rstd_ready"], n + 1)
                for t in range(NT):
                    ins = nc.vector.tensor_scalar(xn[:, NT * b + t, :], x[:, NT * b + t, :], mv[:, b, t, 0:1],
                                                  rstd[:, b, t:t + 1], ALU.subtract, ALU.mult)
                ins.then_inc(q["xn_ready"], 1)

            def key_split(L):
                dve.wait_ge(q["kt_put"], L + 1)
                if L == 0:
                    dve.wait_ge(q["consts_in"], 48)
                    link(nc.vector.tensor_copy(kf[:, :], m0[:, 0:B * MP]))
                else:
                    dve.wait_ge(q["mask_in"], 32)
                    link(nc.vector.memset(cmask[:, :, M:MP], 0))
                    dve.wait_ge(q["kst_in"], 16 * 12)
                    link(nc.vector.tensor_tensor(kf[:, :], m0[:, 0:B * MP], cmask[:, :, :].rearrange("p b j -> p (b j)"), ALU.mult))
                link(nc.vector.tensor_copy(khi[:, :], kf[:, :]))
                link(nc.vector.tensor_tensor(klo[:, :], kf[:, :], khi[:, :].bitcast(F32), ALU.subtract))
                for half, src in enumerate((khi, klo)):
                    for hh_ in range(HG):
                        ins = nc.vector.tensor_scalar(kbd[:, half, :, hh_], src[:, :].bitcast(F32), kmask[:, hh_:hh_ + 1], None, ALU.mult)
                ins.then_inc(q["k_split"], 1)

            def v_blocks(L):
                vm = vmask[:, :].unsqueeze(1).unsqueeze(3)
                for b in range(B):
                    n = B * L + b
                    dve.wait_ge(q["vr_put"], n + 1)
                    src = (tok[0], tok[1], key[0], key[1])[b][0:PR, 0:NC * D].rearrange("p (c h d) -> p c h d", c=NC, h=H)
                    dst = vbd[:, L, b].rearrange("p c (h w) -> p c h w", h=H)
                    nc.vector.tensor_tensor(dst[:, :, :, 0:HD], src, vm.broadcast_to([PR, NC, H, HD]), ALU.mult)
                    nc.vector.tensor_copy(dst[:, :, :, HD:VW], vm.broadcast_to([PR, NC, H, 1])).then_inc(q["v_set"], 1)

            def extra_mask():
                dve.wait_ge(q["mask_in"], 32)
                dve.wait_ge(q["krow_set"], B)
                row = kextra[96:97, :].rearrange("p (b j h) -> p b j h", b=B, h=HG)
                for hh_ in range(HG):
                    ins = nc.vector.tensor_scalar(row[:, :, 0:M, hh_], cmask[96:97, :, 0:M], -1.0, -NEG, ALU.add, ALU.mult)
                ins.then_inc(q["extra_ready"], 1)

            def quant_prep():
                dve.wait_ge(q["wffn_in"], 80)
                link(nc.vector.memset(wmx[:, :], 1.0))
                for j, w in ((0, wg0), (3, wu0)):
                    nc.vector.tensor_reduce(wmx[:, j:j + 2], w[:, 0:2, :], AX.X, ALU.max, apply_absolute_value=True)
                    nc.vector.tensor_reduce(wmx[0:IT[2], j + 2:j + 3], w[0:IT[2], 2, :], AX.X, ALU.max, apply_absolute_value=True)
                link(nc.vector.tensor_reduce(wmx[:, 6:7], wd0[:, :], AX.X, ALU.max, apply_absolute_value=True))
                link(nc.vector.tensor_scalar(wmx[:, :], wmx[:, :], 1.0 / QMAX, None, ALU.mult))
                link(nc.vector.reciprocal(rwm[:, :], wmx[:, :]))
                for j, w in ((0, wg0), (3, wu0)):
                    for t in range(3):
                        ins = nc.vector.tensor_scalar(w[0:IT[t], t, :], w[0:IT[t], t, :], rwm[0:IT[t], j + t:j + t + 1], MAGIC, ALU.mult, ALU.add)
                ins = nc.vector.tensor_scalar(wd0[:, :], wd0[:, :], rwm[:, 6:7], MAGIC, ALU.mult, ALU.add)
                ins.then_inc(q["wq_rounded"], 1)
                nc.vector.tensor_scalar(diag[:, :], ident[:, :], wmx[:, 6:7], None, ALU.mult).then_inc(q["sd_diag"], 1)
                dve.wait_ge(q["csc_ready"], 1)
                link(nc.vector.tensor_scalar(eclip[:, :], eclip[:, :], 1.0, None, ALU.add))
                link(nc.vector.reciprocal(csc[:, :], eclip[:, :]))
                link(nc.vector.tensor_scalar(csc[:, :], csc[:, :], 1.0 / QMAX, None, ALU.mult))
                dve.wait_ge(q["sd_put"], 1)
                nc.vector.tensor_copy(sdrow[:, :], key[1][:, 0:D]).then_inc(q["sd_copied"], 1)

            def attention(L):
                for i, k in steps(-2, B):
                    u = B * L + i
                    if i + 1 in UNITS:
                        n = 16 * (u + 1) + k
                        v = u + 1
                        t, g = divmod(k, G)
                        dve.wait_ge(q["tok_put"], n + 1)
                        if k == 0 and v >= 2:
                            dve.wait_ge(q["mt_put"], v - 1)
                        nc.vector.tensor_reduce(mx[:, v % 2, t, HG * g:HG * g + HG],
                                                tok[n % 2][:, 0:KG].rearrange("p (j h) -> p h j", h=HG), AX.X, ALU.max).then_inc(q["tok_maxed"], 1)
                    j, g, t = pv_turn(i, k)
                    if j in UNITS and t == NT - 1:
                        v = B * L + j
                        n = G * v + g
                        dve.wait_ge(q["o_put"], n + 1)
                        o = acc[n % 2][:, 0:NT * HG * VW].rearrange("p (t h w) -> p t h w", t=NT, h=HG)
                        rd = rden[:, n % 2, :].rearrange("p (t h) -> p t h", t=NT)
                        link(nc.vector.reciprocal(rd, o[:, :, :, HD]))
                        if v >= 2:
                            dve.wait_ge(q["ot_put"], v - 1)
                        nc.vector.tensor_tensor(on[:, v % 2, :, HG * HD * g:HG * HD * g + HG * HD].rearrange("p t (h d) -> p t h d", h=HG),
                                                o[:, :, :, 0:HD], rd.unsqueeze(3).broadcast_to([128, NT, HG, HD]), ALU.mult
                                                ).then_inc(q["o_normed"], 1)
                    if k == AT_WO + 1 and i - 1 in UNITS:
                        b = i - 1
                        dve.wait_ge(q["att_put"], u)
                        if L == 0:
                            dve.wait_ge(q["xb_set"], NT * (b + 1))
                        nc.vector.tensor_tensor(x[:, NT * b:NT * b + NT, :], m1[:, :].rearrange("p (t d) -> p t d", t=NT),
                                                x[:, NT * b:NT * b + NT, :], ALU.add).then_inc(q["x_attended"], 1)
                        dve.wait_ge(q["x_attended"], B * L + b + 1)
                        ln_stats(B * (2 * L + 1) + b)
                    if k == AT_Q + 1 and i + 2 in UNITS:
                        v = u + 2
                        dve.wait_ge(q["q_hi"], v + 1)
                        if v >= 2:
                            dve.wait_ge(stack_q[v % 2], STQ * (v // 2))
                        nc.vector.scalar_tensor_tensor(qlo[:, v % 2, :], m1[:, :], bq[:, L:L + 1], qhi[:, v % 2, :].bitcast(F32),
                                                       ALU.add, ALU.subtract).then_inc(q["q_lo"], 1)
                    if k == AT_LN and i - 1 in UNITS:
                        n = B * (2 * L + 1) + i - 1
                        ln_apply(n)
                        if L == 0:
                            dve.wait_ge(q["xn_ready"], n + 1)
                            b = n % B
                            nc.vector.tensor_reduce(axb[:, 0, b:b + 1], xn[:, NT * b:NT * b + NT, :], AX.XY, ALU.max, apply_absolute_value=True)
                    if k == 15 and i + 1 in UNITS:
                        v = u + 1
                        dve.wait_ge(q["mt_hi"], v + 1)
                        if v >= 2:
                            dve.wait_ge(stack_m[v % 2], STM * (v // 2))
                        nc.vector.tensor_tensor(mtlo[:, v % 2, :], m0[0:H, :], mthi[:, v % 2, :].bitcast(F32), ALU.subtract).then_inc(q["mt_lo"], 1)
                    if L == 0 and i == -1 and k == 15:
                        quant_prep()
                        extra_mask()
                        key_split(1)
                        v_blocks(1)

            def whole_max(j):
                dve.wait_ge(q["const_set"], 1)
                link(nc.vector.memset(gm1[0:1, j:j + 1], 0.0))
                nc.vector.tensor_reduce(axm[:, j:j + 1], axb[:, j, :], AX.X, ALU.max).then_inc(q["part_max"], 1)
                dve.wait_ge(q["row_put"], j + 1)
                nc.vector.tensor_reduce(gm1[0:1, j:j + 1], m1[0:1, 0:128], AX.X, ALU.max).then_inc(q["row_max"], 1)
                dve.wait_ge(q["bc_put"], j + 1)
                link(nc.vector.tensor_scalar(qs[:, j:j + 1], m1[:, 256:257], csc[:, j:j + 1], None, ALU.mult))
                link(nc.vector.reciprocal(rqs[:, j:j + 1], qs[:, j:j + 1]))

            for b in range(B):
                dve.wait_ge(x_in[b], 16)
                ln_stats(b)
                if b == 0:
                    ln_apply(0)
                    key_split(0)
            for b in range(1, B):
                ln_apply(b)
            v_blocks(0)
            attention(0)
            if STOP > 1:
                whole_max(0)
                nc.vector.memset(h0[96:128, :, 2, :], 0.0)
                for j in range(2):
                    nc.vector.tensor_scalar(gus[:, 3 * j:3 * j + 2], wmx[:, 3 * j:3 * j + 2], qs[:, 0:1], None, ALU.mult)
                    nc.vector.tensor_scalar(gus[0:IT[2], 3 * j + 2:3 * j + 3], wmx[0:IT[2], 3 * j + 2:3 * j + 3], qs[0:IT[2], 0:1], None, ALU.mult)
                for b in range(B):
                    v = xn[:, NT * b:NT * b + NT, :]
                    link(nc.vector.tensor_scalar(v, v, rqs[:, 0:1], QMAX, ALU.mult, ALU.min))
                    nc.vector.tensor_scalar(v, v, -QMAX - 1.0, MAGIC, ALU.max, ALU.add).then_inc(q["xq_ready"], 1)
                for n in range(3 * B):
                    b, i3 = divmod(n, 3)
                    w = IT[i3]
                    dve.wait_ge(q["silu_ready"], n + 1)
                    dve.wait_ge(q["u_put"], n + 1)
                    nc.vector.scalar_tensor_tensor(h0[0:w, b, i3, :], key[n % 2][0:w, :], gus[0:w, 3 + i3:4 + i3],
                                                   sg[0:w, n % 2, :], ALU.mult, ALU.mult).then_inc(q["h_ready"], 1)
                    if i3 == 2:
                        dve.wait_ge(q["h_ready"], n + 1)
                        link(nc.vector.tensor_reduce(axb[:, 1, b:b + 1], h0[:, b, :, :], AX.XY, ALU.max, apply_absolute_value=True))
                whole_max(1)
                for b in range(B):
                    v = h0[:, b, :, :]
                    link(nc.vector.tensor_scalar(v, v, rqs[:, 1:2], QMAX, ALU.mult, ALU.min))
                    nc.vector.tensor_scalar(v, v, -QMAX - 1.0, MAGIC, ALU.max, ALU.add).then_inc(q["hq_f"], 1)
                    if b == 0:
                        link(nc.vector.tensor_scalar(sdrow[:, :], sdrow[:, :], qs[:, 1:2], None, ALU.mult))
                for b in range(B):
                    dve.wait_ge(q["d_put"], b + 1)
                    link(nc.vector.tensor_tensor(dtmp[:, b % 2, :].rearrange("p (t d) -> p t d", t=NT),
                                                 (m0, m1)[b % 2][:, :].rearrange("p (t d) -> p t d", t=NT),
                                                 sdrow[:, :].unsqueeze(1).broadcast_to([128, NT, D]), ALU.mult))
                    v = x[:, NT * b:NT * b + NT, :]
                    nc.vector.tensor_tensor(v, v, dtmp[:, b % 2, :].rearrange("p (t d) -> p t d", t=NT), ALU.add).then_inc(q["x_ffn"], 1)
                    dve.wait_ge(q["x_ffn"], b + 1)
                    ln_stats(2 * B + b)
                    ln_apply(2 * B + b)
            if STOP > 2:
                attention(1)
            if STOP > 3:
                dve.wait_ge(q["gate_in"], 80)
                link(nc.vector.tensor_copy(gwh[:, :], gwf[:, :]))
                nc.vector.tensor_tensor(gwl[:, :], gwf[:, :], gwh[:, :].bitcast(F32), ALU.subtract)
                nc.vector.tensor_reduce(b2s[:, :], b2[:, :], AX.X, ALU.add).then_inc(q["b2_summed"], 1)

                def x_lo(b):
                    dve.wait_ge(q["x1_hi"], b + 1)
                    if b >= 2:
                        dve.wait_ge(q["w1_put"], NH * (b - 1))
                    nc.vector.tensor_tensor(xl1[:, b % 2, :], m0[:, :], xh1[:, b % 2, :].bitcast(F32), ALU.subtract).then_inc(q["x1_lo"], 1)

                def bc(ap):
                    return ap.unsqueeze(2).broadcast_to([128, NT, E])

                def gate_a(b):
                    dve.wait_ge(q["lg_put"], b + 1)
                    if b >= 1:
                        dve.wait_ge(q["lg_e"], b)
                    link(nc.vector.tensor_tensor(lg[:, :, :], m1[:, 0:NT * E].rearrange("p (t e) -> p t e", t=NT),
                                                 gb[:, :].unsqueeze(1).broadcast_to([128, NT, E]), ALU.add))
                    link(nc.vector.tensor_tensor(lq[:, :, :], lg[:, :, :], lg[:, :, :], ALU.mult))
                    nc.vector.tensor_reduce(s4[:, 0, :], lq[:, :, :], AX.X, ALU.add).then_inc(q["lg_ms"], 1)

                def gate_b(b):
                    dve.wait_ge(q["lg_r"], b + 1)
                    link(nc.vector.tensor_tensor(lg[:, :, :], lg[:, :, :], bc(s4[:, 2, :]), ALU.mult))
                    link(nc.vector.tensor_tensor(lg[:, :, :], lg[:, :, :], rw[:, :].unsqueeze(1).broadcast_to([128, NT, E]), ALU.mult))
                    link(nc.vector.tensor_scalar(lg[:, :, :], lg[:, :, :], 2.0, None, ALU.mult))
                    link(nc.vector.tensor_reduce(s4[:, 3, :], lg[:, :, :], AX.X, ALU.max))
                    nc.vector.tensor_tensor(lg[:, :, :], lg[:, :, :], bc(s4[:, 3, :]), ALU.subtract).then_inc(q["lg_d"], 1)

                def gate_c(b):
                    dve.wait_ge(q["lg_e"], b + 1)
                    link(nc.vector.tensor_reduce(s4[:, 4, :], lq[:, :, :], AX.X, ALU.add))
                    link(nc.vector.reciprocal(s4[:, 4, :], s4[:, 4, :]))
                    link(nc.vector.tensor_scalar(s4[:, 3, :], s4[:, 4, :], 1e-6, None, ALU.add))
                    link(nc.vector.reciprocal(s4[:, 3, :], s4[:, 3, :]))
                    link(nc.vector.tensor_tensor(ng[:, b % 2, :], s4[:, 4, :], s4[:, 3, :], ALU.mult))

                x_lo(0)
                for n in range(NH * B + 6):
                    if n < NH * B:
                        dve.wait_ge(q["gelu_ready"], n + 1)
                        if n >= 3:
                            dve.wait_ge(q["w2_done"], n - 2)
                        nc.vector.tensor_copy(hh[:, n % 3, :], hf[:, n % 3, :]).then_inc(q["h_split"], 1)
                        dve.wait_ge(q["h_split"], 2 * n + 1)
                        nc.vector.tensor_tensor(hl[:, n % 3, :], hf[:, n % 3, :], hh[:, n % 3, :].bitcast(F32), ALU.subtract).then_inc(q["h_split"], 1)
                    b = n // NH
                    if n % NH == 8 and b + 1 < B:
                        x_lo(b + 1)
                    if n % NH == 10 and b < B:
                        gate_a(b)
                    if n % NH == 12 and b < B:
                        gate_b(b)
                    if n % NH == 14 and b < B:
                        gate_c(b)
                    if n % NH == 5 and b >= 1:
                        v = b - 1
                        dve.wait_ge(q["yT_put"], v + 1)
                        for t in range(NT):
                            ins = nc.vector.scalar_tensor_tensor(xn[:, NT * v + t, :], m1[:, 128 * t:128 * t + 128],
                                                                 ng[:, v % 2, t:t + 1], x[:, NT * v + t, :], ALU.mult, ALU.add)
                        ins.then_inc(q["y_done"], 1)
            else:
                for b in range(B):
                    nc.vector.tensor_copy(xn[:, NT * b:NT * b + NT, :], x[:, NT * b:NT * b + NT, :]).then_inc(q["y_done"], 1)

        @block.tensor
        def _(pe):
            mm = nc.tensor.matmul

            def keys_values(L):
                if L == 0:
                    pe.wait_ge(q["ctx_in"], 32)
                    pe.wait_ge(q["watt_in"], 80)
                    pe.wait_ge(q["ctxr_ready"], 1)
                else:
                    pe.wait_ge(q["wqT_copied"], 4)
                    pe.wait_ge(q["mt_lo"], 1)
                    pe.wait_ge(q["tok_maxed"], 16)
                    pe.wait_ge(q["sd_copied"], 1)
                mm(m0[:, 0:B * MP], wk[:, L, :], ctxt[:, :], start=True, stop=True).then_inc(q["kt_put"], 1)
                for b in range(B):
                    if L == 1 and b == 3:
                        pe.wait_ge(q["kt_put"], 2)
                    bank = (tok[0], tok[1], key[0], key[1])[b]
                    for c in range(NC):
                        lo = b * MP + c * JC
                        ins = mm(bank[0:PR, D * c:D * c + D], ctxr[:, lo:lo + JC, :].rearrange("p j h -> p (j h)"), wv[:, L, :], start=True, stop=True)
                    ins.then_inc(q["vr_put"], 1)

            def quant_prep():
                pe.wait_ge(q["wq_rounded"], 1)
                pe.wait_ge(q["tok_maxed"], 16)
                for n, w in enumerate((wg0, wu0)):
                    for t in range(3):
                        ins = nc.tensor.transpose(tok[n][:, 128 * t:128 * t + IT[t]], w[0:IT[t], t, :], ident[0:IT[t], 0:IT[t]])
                    ins.then_inc(q["wqT_put"], 1)
                for t in range(3):
                    ins = nc.tensor.transpose(key[0][0:IT[t], 128 * t:128 * t + 128], wd0[:, 128 * t:128 * t + IT[t]], ident[:, :])
                ins.then_inc(q["wqT_put"], 1)
                pe.wait_ge(q["sd_diag"], 1)
                pe.wait_ge(q["const_set"], 1)
                mm(key[1][:, 0:D], ones[:, :], diag[:, :], start=True, stop=True).then_inc(q["sd_put"], 1)

            def attention(L):
                for i, k in steps(-2, B):
                    u = B * L + i
                    if i + 1 in UNITS:
                        v = u + 1
                        s, n = v % 2, 16 * v + k
                        t, g = divmod(k, G)
                        if k == 0:
                            pe.wait_ge(stack_q[s], STQ * (v // 2 + 1))
                            if i + 1 == 0:
                                pe.wait_ge(q["kst_in"], 192 * (L + 1))
                                pe.wait_ge(q["krow_set"], B * (L + 1))
                                pe.wait_ge(q["const_set"], 1)
                                pe.wait_ge(q["v_set"], B * (L + 1))
                        if n >= 2:
                            pe.wait_ge(q["tok_maxed"], n - 1)
                        mm(tok[n % 2][:, 0:KG], qst[0:MASKROW + 1, s, g, 128 * t:128 * t + 128], kst[0:MASKROW + 1, i + 1, g, :],
                           start=True, stop=True).then_inc(q["tok_put"], 1)
                    j, g, t = pv_turn(i, k)
                    if j in UNITS:
                        v = B * L + j
                        n = G * v + g
                        if t == 0:
                            pe.wait_ge(q["p_ready"], 12 * v + NC * (g + 1))
                            if n >= 2:
                                pe.wait_ge(q["o_normed"], n - 1)
                        lo = HG * VW * t
                        for c in range(NC):
                            ins = mm(acc[n % 2][:, lo:lo + HG * VW], p[:, NC * g + c, 128 * t:128 * t + 128],
                                     vbd[:, L, j, c, HG * VW * g:HG * VW * g + HG * VW], start=(c == 0), stop=(c == NC - 1))
                        if t == NT - 1:
                            ins.then_inc(q["o_put"], 1)
                    if i in UNITS and k >= LAG:
                        n = 12 * u + k - LAG
                        g, c = divmod(k - LAG, NC)
                        s = u % 2
                        if k == LAG:
                            pe.wait_ge(stack_m[s], STM * (u // 2 + 1))
                        if n >= 2:
                            pe.wait_ge(q["p_ready"], n - 1)
                        mm(key[n % 2][0:PR, :], kst[0:KROWS, i, g, PR * c:PR * c + PR], qst[0:KROWS, s, g, :],
                           start=True, stop=True).then_inc(q["key_put"], 1)
                    if k == AT_OT and i - 1 in UNITS:
                        v = u - 1
                        pe.wait_ge(q["o_normed"], G * (v + 1))
                        m0_free(i, L)
                        for t in range(NT):
                            ins = nc.tensor.transpose(m0[:, 128 * t:128 * t + 128], on[:, v % 2, t, :], ident[:, :])
                        ins.then_inc(q["ot_put"], 1)
                        n_ot[0] += 1
                    if k == AT_XT and i + 2 in UNITS:
                        v = u + 2
                        pe.wait_ge(q["xn_ready"], 2 * B * L + i + 3)
                        m0_free(i, L)
                        if v == 0:
                            pe.wait_ge(q["consts_in"], 48)
                            pe.wait_ge(q["k_split"], 1)
                        for t in range(NT):
                            ins = nc.tensor.transpose(m0[:, 128 * t:128 * t + 128], xn[:, NT * (i + 2) + t, :], ident[:, :])
                        ins.then_inc(q["xt_put"], 1)
                        n_xt[0] += 1
                    if k == AT_WO and i - 1 in UNITS:
                        v = u - 1
                        pe.wait_ge(q["ot_copied"], v + 1)
                        m1_free()
                        for t in range(NT):
                            ins = mm(m1[:, 128 * t:128 * t + 128], ot[:, v % 2, 128 * t:128 * t + 128], wo[:, L, :], start=True, stop=True)
                        ins.then_inc(q["att_put"], 1)
                        n_wo[0] += 1
                    if k == AT_Q and i + 2 in UNITS:
                        v = u + 2
                        pe.wait_ge(q["xt_copied"], v + 1)
                        m1_free()
                        mm(m1[:, :], wq[:, L, :], xt[:, v % 2, :], start=True, stop=True).then_inc(q["q_put"], 1)
                        n_q[0] += 1
                    if k == 15 and i + 1 in UNITS:
                        v = u + 1
                        pe.wait_ge(q["tok_maxed"], 16 * (v + 1))
                        m0_free(i, L)
                        for t in range(NT):
                            ins = nc.tensor.transpose(m0[0:H, 128 * t:128 * t + 128], mx[:, v % 2, t, :], ident[:, :])
                        ins.then_inc(q["mt_put"], 1)
                        n_mt[0] += 1
                    if L == 0 and i == -1 and k == 15:
                        quant_prep()
                        keys_values(1)
                        pe.wait_ge(q["k_split"], 2)
                        pe.wait_ge(q["v_set"], 2 * B)

            n_ot, n_xt, n_mt, n_wo, n_q = [0], [0], [0], [0], [0]

            def m0_free(i, L):
                for count, name in ((n_ot, "ot_copied"), (n_xt, "xt_copied"), (n_mt, "mt_lo")):
                    if count[0]:
                        pe.wait_ge(q[name], count[0])

            def m1_free():
                for count, name in ((n_wo, "x_attended"), (n_q, "q_lo")):
                    if count[0]:
                        pe.wait_ge(q[name], count[0])

            def whole_max(j):
                pe.wait_ge(q["part_max"], j + 1)
                mm(m1[0:1, 0:128], axm[:, j:j + 1], ident[:, :], start=True, stop=True).then_inc(q["row_put"], 1)
                pe.wait_ge(q["row_max"], j + 1)
                mm(m1[:, 256:257], ones[0:1, :], gm1[0:1, j:j + 1], start=True, stop=True).then_inc(q["bc_put"], 1)

            keys_values(0)
            attention(0)
            if STOP > 1:
                whole_max(0)
                for b in range(B):
                    pe.wait_ge(q["xq_ready"], b + 1)
                    if b >= 2:
                        pe.wait_ge(q["xqt_copied"], b - 1)
                    for t in range(NT):
                        ins = nc.tensor.transpose((m0, m1)[b % 2][:, 128 * t:128 * t + 128], xn[:, NT * b + t, :], ident[:, :])
                    ins.then_inc(q["xqt_put"], 1)
                for n in range(3 * B):
                    b, i3 = divmod(n, 3)
                    w, lo = IT[i3], 128 * i3
                    pe.wait_ge(q["xqt_copied"], b + 1)
                    if n >= 2:
                        pe.wait_ge(q["silu_ready"], n - 1)
                    mm(tok[n % 2][0:w, :], wgT[:, lo:lo + w], xqt[:, b, :], start=True, stop=True).then_inc(q["g_put"], 1)
                    if n >= 2:
                        pe.wait_ge(q["h_ready"], n - 1)
                    mm(key[n % 2][0:w, :], wuT[:, lo:lo + w], xqt[:, b, :], start=True, stop=True).then_inc(q["u_put"], 1)
                whole_max(1)
                for b in range(B):
                    pe.wait_ge(q["hq_ready"], b + 1)
                    if b >= 2:
                        pe.wait_ge(q["x_ffn"], b - 1)
                    for t in range(NT):
                        for i3 in range(3):
                            w = IT[i3]
                            ins = mm((m0, m1)[b % 2][:, 128 * t:128 * t + 128], hq[0:w, b, i3, 128 * t:128 * t + 128], wdT[0:w, i3, :],
                                     start=(i3 == 0), stop=(i3 == 2))
                    ins.then_inc(q["d_put"], 1)
            if STOP > 2:
                pe.wait_ge(q["x_ffn"], B)
                attention(1)
            if STOP > 3:
                ring = tok + key

                def x_transposed(b):
                    pe.wait_ge(q["xn_ready"], 3 * B + b + 1)
                    if b == 0:
                        pe.wait_ge(q["ot_copied"], 2 * B)
                    else:
                        pe.wait_ge(q["x1_lo"], b)
                    for t in range(NT):
                        ins = nc.tensor.transpose(m0[:, 128 * t:128 * t + 128], xn[:, NT * b + t, :], ident[:, :])
                    ins.then_inc(q["xt1_put"], 1)

                def logits(b):
                    pe.wait_ge(q["x1_lo"], b + 1)
                    if b == 0:
                        pe.wait_ge(q["b2_summed"], 1)
                        pe.wait_ge(q["x_attended"], 2 * B)
                    if b >= 2:
                        pe.wait_ge(q["y_done"], b - 1)
                    for t in range(NT):
                        tt = slice(128 * t, 128 * t + 128)
                        pairs = [(xh, gw_) for xh in (xh1, xl1) for gw_ in (gwh, gwl)]
                        for j, (xs, gs) in enumerate(pairs):
                            ins = mm(m1[:, E * t:E * t + E], xs[:, b % 2, tt], gs[:, :], start=(j == 0), stop=(j == 3))
                    ins.then_inc(q["lg_put"], 1)

                x_transposed(0)
                logits(0)
                pe.wait_ge(q["w1_split"], 1)
                pe.wait_ge(q["w2_split"], 1)
                for n in range(NH * B + 5):
                    b, j = divmod(n, NH)
                    if n < NH * B:
                        w = slice(128 * j, 128 * j + 128)
                        bank = ring[n % 4]
                        if n >= 4:
                            pe.wait_ge(q["gelu_ready"], n - 3)
                        if j == 0:
                            pe.wait_ge(q["x1_lo"], b + 1)
                        mm(bank[:, :], w1l[:, w], xh1[:, b % 2, :], start=True, stop=False)
                        mm(bank[:, :], w1h[:, w], xl1[:, b % 2, :], start=False, stop=False)
                        mm(bank[:, :], w1h[:, w], xh1[:, b % 2, :], start=False, stop=True).then_inc(q["w1_put"], 1)
                    m = n - 2
                    if 0 <= m < NH * B:
                        bm, jm = divmod(m, NH)
                        w = slice(128 * jm, 128 * jm + 128)
                        pe.wait_ge(q["h_split"], 2 * m + 2)
                        if jm == 0 and bm >= 2:
                            pe.wait_ge(q["yt_copied"], bm - 1)
                        mm(acc[bm % 2][:, :], w2l[:, w], hh[:, m % 3, :], start=(jm == 0), stop=False)
                        mm(acc[bm % 2][:, :], w2h[:, w], hl[:, m % 3, :], start=False, stop=False)
                        mm(acc[bm % 2][:, :], w2h[:, w], hh[:, m % 3, :], start=False, stop=(jm == NH - 1)).then_inc(q["w2_done"], 1)
                    if j == 8 and b + 1 < B:
                        x_transposed(b + 1)
                    if j == 4 and b >= 1:
                        v = b - 1
                        pe.wait_ge(q["yt_copied"], v + 1)
                        pe.wait_ge(q["lg_ms"], v + 1)
                        for t in range(NT):
                            ins = nc.tensor.transpose(m1[:, 128 * t:128 * t + 128], yt[:, 128 * t:128 * t + 128], ident[:, :])
                        ins.then_inc(q["yT_put"], 1)
                    if j == 9 and 1 <= b < B:
                        pe.wait_ge(q["y_done"], b)
                        logits(b)


ONE = np.float32(1.0)


def shape_constants():
    ident = np.eye(128, dtype=np.float32)
    d = np.arange(128)
    kmask = ((d // HD % HG)[:, None] == np.arange(HG)[None]).astype(np.float32)
    vmask = ((np.arange(PR) % HG)[:, None] == (np.arange(H) % HG)[None]).astype(np.float32)
    rows = np.zeros((KROWS - 96, B, MP, HG), np.float32)
    rows[0, :, M:, :] = NEG
    for h in range(HG):
        rows[MHI - 96 + h, :, :, h] = -1.0
        rows[MLO - 96 + h, :, :, h] = -1.0
    return ident, kmask, vmask, rows.reshape(KROWS - 96, B * KG)


def kernel(**inputs):
    import concourse.bacc as _bacc
    from concourse.bass_utils import run_bass_kernel_spmd as _run

    v = {k: np.asarray(w) for k, w in inputs.items()}
    ident, kmask, vmask, rows = shape_constants()
    kv = v["L0_xattn_Wkv"].reshape(H, 2, HD, C)
    bkv = v["L0_xattn_bkv"].reshape(H, 2, HD)
    zero = np.zeros((1, D), np.float32)
    ctx = np.zeros((C, B, MP), np.float32)
    ctx[:, :, 0:M] = v["ctx_768"].transpose(2, 0, 1)
    arrays = {
        "x": v["x"],
        "ident": ident, "kmask": kmask, "vmask": vmask, "krows": rows,
        "ones_row": np.ones((1, B * MP), np.float32),
        "ctxT": ctx,
        "mask": v["mask_BxS2_bf1"].view(np.uint8),
        "wk": np.stack([np.concatenate([kv[:, 0].reshape(D, C).T, bkv[:, 0].reshape(1, D)]),
                        np.concatenate([v["L1_xattn_Wk"], zero])], 1),
        "wv": np.stack([np.concatenate([kv[:, 1].reshape(D, C).T, bkv[:, 1].reshape(1, D)]),
                        np.concatenate([v["L1_xattn_Wv"], zero])], 1),
        "wq": np.stack([v["L0_xattn_Wq"].T, v["L1_xattn_Wq"]], 1),
        "wo": np.stack([v["L0_xattn_Wo"].T, v["L1_xattn_Wo"]], 1),
        "bq": v["L0_xattn_bq"].reshape(D, 1),
        "bo": v["L0_xattn_bo"],
        "clip": np.concatenate([v["L0_ffn_clip_x"], v["L0_ffn_clip_down"]]),
        "w_gate": v["L0_ffn_w_gate"], "w_up": v["L0_ffn_w_up"], "w_down": v["L0_ffn_w_down"],
        "gate_wT": v["L1_ffn_gate_w"].T, "gate_b": v["L1_ffn_gate_b"], "rms_w": v["L1_ffn_rms_w"],
        "w1": v["L1_ffn_w1"], "b1": v["L1_ffn_b1"].reshape(NH, 128).T,
        "w2": v["L1_ffn_w2"], "b2": v["L1_ffn_b2"].T,
    }
    nc = _bacc.Bacc("TRN2", target_bir_lowering=False, num_devices=1)
    feeds, aps = {}, {}
    for name, w in arrays.items():
        w = np.ascontiguousarray(w)
        feeds["in_" + name] = w
        aps[name] = nc.dram_tensor("in_" + name, w.shape, mybir.dt.from_np(w.dtype), kind="ExternalInput").ap()
    out = nc.dram_tensor("out_0", (B, S, D), F32, kind="ExternalOutput").ap()
    build(nc, aps, out)
    r = _run(nc, [feeds], core_ids=[0])
    return r.results[0]["out_0"]
```

```python
from contextlib import ExitStack

import numpy as np

import concourse.bass as bass
from concourse import mybir

F32 = mybir.dt.float32
F32R = mybir.dt.float32r
BF16 = mybir.dt.bfloat16
U8 = mybir.dt.uint8
ALU = mybir.AluOpType
ACT = mybir.ActivationFunctionType
AX = mybir.AxisListType

B, S, D = 4, 512, 128
NT = S // 128
M, MP = 77, 78
C = 96
H, HD = 16, 8
G, HG = 4, 4
NC = 3
JC = MP // NC
PR = JC * HG
KG = MP * HG
MASKROW, MHI, MLO, KROWS = 96, 97, 101, 105
I0 = 352
IT = [128, 128, 96]
E, HE = 8, 256
NH = E * HE // 128
STQ, STM = 16 * 3 * G, 16 * G
SCALE = float(HD) ** -0.5
NEG = -(2.0 ** 127)
MAGIC = 1.5 * 2.0 ** 23
QMAX = 127.0
LN_EPS = 1e-5
EPS32 = float(np.finfo(np.float32).eps)
STOP = 9


def build(nc, a, out):
    with ExitStack() as ctx:
        def sb(name, shape, dt=F32):
            return ctx.enter_context(nc.sbuf_tensor(name, shape, dt))

        def ps(name):
            return ctx.enter_context(nc.psum_tensor(name, [128, 512], F32))

        def sem(name):
            return ctx.enter_context(nc.semaphore(name))

        x = sb("x", [128, B * NT, D])
        xn = sb("xn", [128, B * NT, D])
        stats = sb("stats", [128, B, NT, 6])
        mv = sb("mv", [128, B, NT, 2])
        veps = sb("veps", [128, B, NT])
        rstd = sb("rstd", [128, B, NT])
        mhalf = sb("mhalf", [128, NT * E])
        ebase = sb("ebase", [128, NT * E])
        cst = sb("cst", [128, 133 + HG * HD])
        ident = cst[:, 0:128]
        magic = sb("magic", [128, 1])
        ctxt = sb("ctxt", [C + 1, B * MP])
        wkv = sb("wkv", [C + 1, 4, D])
        wk, wv = wkv[:, 0:2, :], wkv[:, 2:4, :]
        wqo = sb("wqo", [D, 4, D])
        wq, wo = wqo[:, 0:2, :], wqo[:, 2:4, :]
        bq = sb("bq", [D, 2])
        bo = sb("bo_sb", [128, D])
        kmask = cst[:, 128:128 + HG]
        mpart = cst[0:2 * H, 132:133]
        vmask = cst[0:PR, 133:133 + HG * HD]
        cmask = sb("cmask", [128, B, MP], U8)
        khi = sb("khi", [D, B * MP], F32R)
        klo = sb("klo", [D, B * MP], F32R)
        rbuf = sb("rbuf", [128, 6 * S], F32R)
        kbd = rbuf[:, 0:2 * B * KG].rearrange("p (s c h) -> p s c h", s=2, h=HG)
        hh = rbuf[:, 0:3 * S].rearrange("p (n c) -> p n c", n=3)
        hl = rbuf[:, 3 * S:6 * S].rearrange("p (n c) -> p n c", n=3)
        kextra = sb("kextra", [128, B * KG])
        kst = sb("kst", [128, B, G, KG], F32R)
        vbd = sb("vbd", [PR, 2, B, NC, D])
        qhi = sb("qhi", [128, 2, S], F32R)
        qlo = sb("qlo", [128, 2, S], F32R)
        qst = sb("qst", [128, 3, G, S], F32R)
        mx = sb("mx", [128, 2, NT, G, 2, HG])
        mthi = sb("mthi", [2 * H, S], F32R)
        mthl = sb("mthl", [2 * H, 2, S], F32R)
        big = sb("big", [128, G * NC * S])
        p = big[0:PR, :].rearrange("p (n c) -> p n c", n=G * NC)
        h0 = big[:, :].rearrange("p (b n c) -> p b n c", b=B, n=3)
        hf = big[:, 0:3 * S].rearrange("p (n c) -> p n c", n=3)
        yt = big[:, 3 * S:4 * S]
        ctxr = big[0:C + 1, 0:B * KG].rearrange("p (j h) -> p j h", h=HG)
        kf = big[:, B * KG:B * KG + B * MP]
        tbuf = sb("tbuf", [128, 6 * S])
        xt = tbuf[:, 0:2 * S].rearrange("p (n c) -> p n c", n=2)
        ov = tbuf[:, 2 * S:3 * S]
        od = tbuf[:, 3 * S:4 * S]
        on = tbuf[:, 4 * S:5 * S].rearrange("p (t d) -> p t d", t=NT)
        ot = tbuf[:, 5 * S:6 * S]
        hq = tbuf[:, :].bitcast(BF16).rearrange("p (b n c) -> p b n c", b=B, n=3)
        sbuf4 = sb("sbuf4", [128, 2 * S])
        sg = sbuf4[:, :].rearrange("p (n c) -> p n c", n=2)
        dtmp = sbuf4[:, :].rearrange("p (n c) -> p n c", n=2)
        rden = sb("rden", [128, NT, H])

        wg0 = sb("wg0", [128, 3, D])
        wu0 = sb("wu0", [128, 3, D])
        wd0 = sb("wd0", [D, I0])
        wmx = sb("wmx", [128, 7])
        rwm = sb("rwm", [128, 7])
        wgT = sb("wgT", [D, I0], BF16)
        wuT = sb("wuT", [D, I0], BF16)
        wdT = sb("wdT", [128, 3, D], BF16)
        clip = sb("clip", [128, 2])
        eclip = sb("eclip", [128, 2])
        csc = sb("csc", [128, 2])
        diag = sb("diag", [D, D])
        sdrow = sb("sdrow", [128, D])
        ones = sb("ones", [128, 128])
        axb = sb("axb", [128, 2, B])
        axm = sb("axm", [128, 2])
        gm1 = sb("gm1", [1, 2])
        qs = sb("qs", [128, 2])
        rqs = sb("rqs", [128, 2])
        gus = sb("gus", [128, 6])
        xqt = sb("xqt", [D, B, S], BF16)

        w1f = sb("w1f", [128, E * HE])
        w1h = sb("w1h", [128, E * HE], F32R)
        w1l = sb("w1l", [128, E * HE], F32R)
        w2h = sb("w2h", [128, NH * D], F32R)
        w2l = sb("w2l", [128, NH * D], F32R)
        b1 = sb("b1", [128, NH])
        b2 = sb("b2", [D, E])
        b2s = sb("b2s", [D, 1])
        gwf = sb("gwf", [D, E])
        gwh = sb("gwh", [D, E], F32R)
        gwl = sb("gwl", [D, E], F32R)
        gb = sb("gb", [128, E])
        rw = sb("rw", [128, E])
        xh1, xl1 = qhi, qlo
        lg = sb("lg", [128, NT, E])
        lq = sb("lq", [128, NT, E])
        s4 = sb("s4", [128, 6, NT])
        ng = sb("ng", [128, 2, NT])

        tok = [ps(f"ps_tok{i}") for i in range(2)]
        key = [ps(f"ps_key{i}") for i in range(2)]
        acc = [ps(f"ps_acc{i}") for i in range(2)]
        m0 = ps("ps_m0")
        m1 = ps("ps_m1")

        x_in = [sem(f"x_in{b}") for b in range(B)]
        s_names = (
            "consts_in bo_in ctx_in wkv_in wqo_in bq_in mask_in wffn_in clip_in w1_in w2_in gate_in "
            "const_set wf_ready extra_ready ctxr_ready kt_put k_split kst_in krow_set vr_put v_set xb_set "
            "var_ready eps_self rstd_ready xn_ready xt_put xt_copied q_put q_hi q_lo "
            "tok_put tok_maxed mt_put mx_doubled mt_hi mt_split key_put p_ready pv_put o_copied on_put o_normed ot_put ot_copied "
            "att_put x_attended dve_self act_self pool_self "
            "wq_rounded wqT_put wqT_copied sd_diag sd_put sd_copied csc_ready "
            "part_max row_put row_max bc_put xq_ready xqt_put xqt_copied g_put u_put silu_ready h_ready "
            "hq_f hq_ready d_put x_ffn w1_split w1_free w2_split b2_summed xt1_put x1_hi x1_lo lg_put lg_ms lg_r lg_d lg_e "
            "ng_ready w1_put gelu_ready h_split w2_done yt_copied yT_put y_done out_done"
        )
        q = {n: sem(n) for n in s_names.split()}
        stack_q = [sem(f"stack_q{i}") for i in range(2)]
        stack_m = [sem(f"stack_m{i}") for i in range(2)]

        block = ctx.enter_context(nc.Block())
        UNITS = range(B)
        AT_XT, AT_DEN, AT_COPY, AT_Q, AT_ON, AT_OT, AT_WO, AT_LN, AT_MAX = 0, 0, 1, 3, 4, 6, 8, 12, 12
        LAG = 2
        PV = {7: (0, 0), 8: (0, 1), 11: (1, 0), 12: (1, 1), 15: (2, 0)}

        def token_turns(k):
            return range(16 * k // 12, 16 * (k + 1) // 12) if k < 12 else ()

        def steps(first_step, last_step):
            for i in range(first_step, last_step + 1):
                for k in range(16):
                    yield i, k

        @block.sync
        def _(sp):
            for b in range(B):
                sp.dma_start(x[:, NT * b:NT * b + NT, :], a["x"][b].rearrange("(t p) d -> p t d", p=128)).then_inc(x_in[b], 16)
                if b == 0:
                    sp.dma_start(wqo[:, :, :], a["wqo"]).then_inc(q["wqo_in"], 16)
            for w, src in ((wg0, a["w_gate"]), (wu0, a["w_up"])):
                sp.dma_start(w[:, 0:2, :], src[0:256, :].rearrange("(t p) d -> p t d", p=128)).then_inc(q["wffn_in"], 16)
                sp.dma_start(w[0:IT[2], 2, :], src[256:I0, :]).then_inc(q["wffn_in"], 16)
            sp.dma_start(wd0[:, :], a["w_down"]).then_inc(q["wffn_in"], 16)

            def stack(dst, src, rows, done):
                for g in range(G):
                    sp.dma_start(dst[:, g, :].bitcast(F32), src[rows * g:rows * g + rows, :].bitcast(F32)).then_inc(done, 16)

            for L in range(2):
                sp.wait_ge(q["k_split"], L + 1)
                if L == 1:
                    sp.wait_ge(q["key_put"], 12 * B)
                for g in range(G):
                    for r, half in enumerate((0, 0, 1)):
                        sp.dma_start(kst[32 * r:32 * r + 32, :, g, :].bitcast(F32),
                                     kbd[32 * g:32 * g + 32, half, :, :].rearrange("p (b j) h -> p b (j h)", b=B).bitcast(F32)
                                     ).then_inc(q["kst_in"], 16)
                for i in range(-2, B):
                    if i + 2 < B:
                        u = B * L + i + 2
                        s = u % 3
                        sp.wait_ge(q["q_hi"], u + 1)
                        if u >= 3:
                            sp.wait_ge(q["key_put"], 12 * (u - 2))
                        for r in (0, 2):
                            stack(qst[32 * r:32 * r + 32, s], qhi[:, u % 2, :], 32, stack_q[u % 2])
                        sp.wait_ge(q["q_lo"], u + 1)
                        stack(qst[32:64, s], qlo[:, u % 2, :], 32, stack_q[u % 2])
                    if 0 <= i + 1 < B:
                        u = B * L + i + 1
                        sp.wait_ge(q["mt_split"], u + 1)
                        stack(qst[MHI:KROWS, u % 3], mthl[:, u % 2, :], 2 * HG, stack_m[u % 2])
            for b in range(B):
                sp.wait_ge(q["y_done"], b + 1)
                sp.dma_start(out[b].rearrange("(t p) d -> p t d", p=128), xn[:, NT * b:NT * b + NT, :]).then_inc(q["out_done"], 16)
            sp.wait_ge(q["out_done"], 16 * B)

        @block.gpsimd
        def _(pool):
            sent = {}

            def done(ins, name):
                sent[name] = sent.get(name, 0) + 1
                ins.then_inc(q[name], 1)
                pool.wait_ge(q[name], sent[name])

            for ap, value in ((mhalf[:, :], -0.5), (ebase[:, :], float(np.e)), (magic[:, :], -MAGIC), (ones[:, :], 1.0),
                              (qst[96:128, :, :, :].bitcast(F32), 1.0), (axb[:, :, :], 0.0)):
                done(nc.gpsimd.memset(ap, value), "pool_self")
            done(nc.gpsimd.memset(bq[:, 1:2], 0.0), "const_set")
            pool.dma_start(gwf[:, :], a["gate_wT"]).then_inc(q["gate_in"], 16)
            pool.dma_start(gb[:, :], a["gate_b"].partition_broadcast(128)).then_inc(q["gate_in"], 16)
            pool.dma_start(rw[:, :], a["rms_w"].partition_broadcast(128)).then_inc(q["gate_in"], 16)
            pool.dma_start(b1[:, :], a["b1"]).then_inc(q["gate_in"], 16)
            pool.dma_start(b2[:, :], a["b2"]).then_inc(q["gate_in"], 16)
            pool.dma_start(w1f[:, :].rearrange("d (e h) -> d e h", e=E), a["w1"].rearrange("e d h -> d e h")).then_inc(q["w1_in"], 16)

            def rstd_of(n):
                b = n % B
                pool.wait_ge(q["var_ready"], n + 1)
                done(nc.gpsimd.tensor_scalar(veps[:, b, :], mv[:, b, :, 1], LN_EPS, None, ALU.add), "eps_self")
                done(nc.gpsimd.tensor_tensor(rstd[:, b, :], veps[:, b, :], mhalf[:, 0:NT], ALU.pow), "rstd_ready")

            for b in range(B):
                rstd_of(b)
            pool.wait_ge(q["bo_in"], 16)
            for b in range(B):
                pool.wait_ge(q["xn_ready"], b + 1)
                for t in range(NT):
                    done(nc.gpsimd.tensor_tensor(x[:, NT * b + t, :], x[:, NT * b + t, :], bo[:, :], ALU.add), "xb_set")
            pool.wait_ge(q["w1_in"], 16)
            done(nc.gpsimd.tensor_copy(w1h[:, :], w1f[:, :]), "pool_self")
            done(nc.gpsimd.tensor_tensor(w1l[:, :], w1f[:, :], w1h[:, :].bitcast(F32), ALU.subtract), "w1_split")
            pool.dma_start(w1f[:, :].rearrange("p (n d) -> p n d", n=NH),
                           a["w2"].rearrange("e (s p) d -> p (e s) d", p=128)).then_inc(q["w2_in"], 16)
            pool.wait_ge(q["w2_in"], 16)
            done(nc.gpsimd.tensor_copy(w2h[:, :], w1f[:, :]), "pool_self")
            done(nc.gpsimd.tensor_tensor(w2l[:, :], w1f[:, :], w2h[:, :].bitcast(F32), ALU.subtract), "w2_split")
            for n in range(B, 3 * B if STOP > 2 else 2 * B if STOP < 2 else 3 * B):
                rstd_of(n)
            if STOP > 2:
                for n in range(3 * B, 4 * B):
                    rstd_of(n)
            if STOP > 3:
                for b in range(B):
                    pool.wait_ge(q["lg_ms"], b + 1)
                    done(nc.gpsimd.tensor_scalar(s4[:, 1, :], s4[:, 0, :], 1.0 / E, EPS32, ALU.mult, ALU.add), "pool_self")
                    done(nc.gpsimd.tensor_tensor(s4[:, 2, :], s4[:, 1, :], mhalf[:, 0:NT], ALU.pow), "lg_r")
                    pool.wait_ge(q["lg_d"], b + 1)
                    done(nc.gpsimd.tensor_tensor(lq[:, :, :], ebase[:, :].rearrange("p (t e) -> p t e", t=NT), lg[:, :, :], ALU.pow), "lg_e")

        @block.scalar
        def _(act):
            act.dma_start(ctxt[:, :], a["ctxT"]).then_inc(q["ctx_in"], 16)
            act.dma_start(wkv[:, :, :], a["wkv"]).then_inc(q["wkv_in"], 16)
            act.dma_start(cst[:, :], a["cst"]).then_inc(q["consts_in"], 16)
            act.dma_start(bq[:, 0:1], a["bq"]).then_inc(q["bq_in"], 16)
            act.dma_start(cmask[:, :, 0:M], a["mask"].partition_broadcast(128)).then_inc(q["mask_in"], 16)
            act.dma_start(kextra[96:KROWS, :], a["krows"]).then_inc(q["mask_in"], 16)
            act.dma_start(bo[:, :], a["bo"].partition_broadcast(128)).then_inc(q["bo_in"], 16)
            act.dma_start(clip[:, :], a["clip"].partition_broadcast(128)).then_inc(q["clip_in"], 16)

            act.wait_ge(q["ctx_in"], 16)
            act.activation(ctxr[:, :, :], ctxt[:, :].unsqueeze(2).broadcast_to([C + 1, B * MP, HG]), ACT.Copy).then_inc(q["ctxr_ready"], 1)
            act.wait_ge(q["mask_in"], 32)

            def key_rows(L):
                r = slice(96, KROWS)
                if L == 1:
                    act.wait_ge(q["extra_ready"], 1)
                    act.wait_ge(q["key_put"], 12 * B)
                for b in range(B):
                    src = kextra[r, b * KG:(b + 1) * KG]
                    act.activation(kst[r, b], src.unsqueeze(1).broadcast_to([KROWS - 96, G, KG]), ACT.Copy).then_inc(q["krow_set"], 1)

            key_rows(0)

            def quant_prep():
                act.wait_ge(q["clip_in"], 16)
                act.activation(eclip[:, :], clip[:, :], ACT.Exp, scale=-1.0).then_inc(q["csc_ready"], 1)
                act.wait_ge(q["const_set"], 1)
                for n, dst in enumerate((wgT, wuT)):
                    act.wait_ge(q["wqT_put"], n + 1)
                    act.activation(dst[:, :], tok[n][:, 0:I0], ACT.Identity, bias=magic[:, 0:1]).then_inc(q["wqT_copied"], 1)
                act.wait_ge(q["wqT_put"], 3)
                act.activation(wdT[:, 0:2, :], key[0][:, 0:256].rearrange("p (t d) -> p t d", t=2), ACT.Identity, bias=magic[:, 0:1]).then_inc(q["wqT_copied"], 1)
                act.activation(wdT[0:IT[2], 2, :], key[0][0:IT[2], 256:384], ACT.Identity, bias=magic[0:IT[2], 0:1]).then_inc(q["wqT_copied"], 1)

            def attention(L):
                for i, k in steps(-2, B):
                    u = B * L + i
                    if i in UNITS and LAG <= k < LAG + 12:
                        j = k - LAG
                        n = 12 * u + j
                        act.wait_ge(q["key_put"], n + 1)
                        if u >= 1:
                            act.wait_ge(q["pv_put"], 3 * (u - 1) + j // G + 1)
                        act.activation(p[:, j, :], key[n % 2][0:PR, :], ACT.Exp, scale=SCALE).then_inc(q["p_ready"], 1)
                    if k == AT_XT and i + 2 in UNITS:
                        v = u + 2
                        act.wait_ge(q["xt_put"], v + 1)
                        if v >= 2:
                            act.wait_ge(q["q_put"], v - 1)
                        act.activation(xt[:, v % 2, :], m0[:, :], ACT.Copy).then_inc(q["xt_copied"], 1)
                    if k == AT_COPY and i - 1 in UNITS:
                        act.wait_ge(q["pv_put"], 3 * u)
                        if u >= 2:
                            act.wait_ge(q["on_put"], u - 1)
                        act.activation(ov[:, :], acc[0][:, :], ACT.Copy)
                        act.activation(od[:, :], acc[1][:, :], ACT.Copy).then_inc(q["o_copied"], 1)
                    if k == AT_Q and i + 2 in UNITS:
                        v = u + 2
                        act.wait_ge(q["q_put"], v + 1)
                        if v >= 2:
                            act.wait_ge(stack_q[v % 2], STQ * (v // 2))
                        if v == 0:
                            act.wait_ge(q["bq_in"], 16)
                            act.wait_ge(q["const_set"], 1)
                        act.activation(qhi[:, v % 2, :], m1[:, :], ACT.Identity, bias=bq[:, L:L + 1]).then_inc(q["q_hi"], 1)
                    if k == AT_OT and i - 1 in UNITS:
                        act.wait_ge(q["ot_put"], u)
                        if u >= 2:
                            act.wait_ge(q["att_put"], u - 1)
                        act.activation(ot[:, :], m0[:, :], ACT.Copy).then_inc(q["ot_copied"], 1)
                    if k == AT_MAX and i + 1 in UNITS:
                        v = u + 1
                        act.wait_ge(q["mt_put"], v + 1)
                        if v >= 1:
                            act.wait_ge(q["mt_split"], v)
                        act.activation(mthi[:, :], m0[0:2 * H, :], ACT.Copy).then_inc(q["mt_hi"], 1)
                    if L == 0 and i == -1 and k == 15:
                        quant_prep()

            attention(0)
            key_rows(1)
            if STOP > 1:
                for b in range(B):
                    act.wait_ge(q["xqt_put"], b + 1)
                    act.activation(xqt[:, b, :], (m0, m1)[b % 2][:, :], ACT.Identity, bias=magic[:, 0:1]).then_inc(q["xqt_copied"], 1)
                for n in range(3 * B):
                    b, i3 = divmod(n, 3)
                    w = IT[i3]
                    act.wait_ge(q["g_put"], n + 1)
                    if n >= 2:
                        act.wait_ge(q["h_ready"], n - 1)
                    act.activation(sg[0:w, n % 2, :], tok[n % 2][0:w, :], ACT.Silu, scale=gus[0:w, i3:i3 + 1]).then_inc(q["silu_ready"], 1)
                for b in range(B):
                    act.wait_ge(q["hq_f"], b + 1)
                    act.activation(hq[:, b, :, :], h0[:, b, :, :], ACT.Identity, bias=magic[:, 0:1]).then_inc(q["hq_ready"], 1)
            if STOP > 2:
                attention(1)
            if STOP > 3:
                def x_hi(b):
                    act.wait_ge(q["xt1_put"], b + 1)
                    if b >= 2:
                        act.wait_ge(q["w1_put"], NH * (b - 1))
                    act.activation(xh1[:, b % 2, :], m0[:, :], ACT.Copy).then_inc(q["x1_hi"], 1)

                x_hi(0)
                for n in range(NH * B + 4):
                    if n < NH * B:
                        act.wait_ge(q["w1_put"], n + 1)
                        if n >= 3:
                            act.wait_ge(q["h_split"], 2 * (n - 2))
                        act.activation(hf[:, n % 3, :], (tok + key)[n % 4][:, :], ACT.Gelu, bias=b1[:, n % NH:n % NH + 1]).then_inc(q["gelu_ready"], 1)
                    if n % NH == 8 and n // NH + 1 < B:
                        x_hi(n // NH + 1)
                    if n % NH == 3 and n >= NH:
                        b = n // NH - 1
                        act.wait_ge(q["w2_done"], NH * (b + 1))
                        if b == 0:
                            act.wait_ge(q["b2_summed"], 1)
                        if b >= 1:
                            act.wait_ge(q["yT_put"], b)
                        act.activation(yt[:, :], acc[b % 2][:, :], ACT.Identity, bias=b2s[:, 0:1]).then_inc(q["yt_copied"], 1)

        @block.vector
        def _(dve):
            link_n = [0]

            def link(ins):
                link_n[0] += 1
                ins.then_inc(q["dve_self"], 1)
                dve.wait_ge(q["dve_self"], link_n[0])

            def ln_stats(n):
                b = n % B
                for t in range(NT):
                    ins = nc.vector.bn_stats(stats[:, b, t, :], x[:, NT * b + t, :])
                link(ins)
                for t in range(NT):
                    ins = nc.vector.bn_aggr(mv[:, b, t, :], stats[:, b, t, :])
                ins.then_inc(q["var_ready"], 1)

            def ln_apply(n):
                b = n % B
                dve.wait_ge(q["rstd_ready"], n + 1)
                for t in range(NT):
                    ins = nc.vector.tensor_scalar(xn[:, NT * b + t, :], x[:, NT * b + t, :], mv[:, b, t, 0:1],
                                                  rstd[:, b, t:t + 1], ALU.subtract, ALU.mult)
                ins.then_inc(q["xn_ready"], 1)

            def key_split(L):
                dve.wait_ge(q["kt_put"], L + 1)
                if L == 0:
                    dve.wait_ge(q["consts_in"], 16)
                    link(nc.vector.tensor_copy(kf[:, :], m0[:, 0:B * MP]))
                else:
                    dve.wait_ge(q["mask_in"], 32)
                    link(nc.vector.memset(cmask[:, :, M:MP], 0))
                    dve.wait_ge(q["kst_in"], 16 * 12)
                    link(nc.vector.tensor_tensor(kf[:, :], m0[:, 0:B * MP], cmask[:, :, :].rearrange("p b j -> p (b j)"), ALU.mult))
                link(nc.vector.tensor_copy(khi[:, :], kf[:, :]))
                link(nc.vector.tensor_tensor(klo[:, :], kf[:, :], khi[:, :].bitcast(F32), ALU.subtract))
                for half, src in enumerate((khi, klo)):
                    for hh_ in range(HG):
                        ins = nc.vector.tensor_scalar(kbd[:, half, :, hh_], src[:, :].bitcast(F32), kmask[:, hh_:hh_ + 1], None, ALU.mult)
                ins.then_inc(q["k_split"], 1)

            def v_blocks(L):
                vm = vmask.unsqueeze(1).broadcast_to([PR, NC * G, HG * HD])
                for b in range(B):
                    n = B * L + b
                    dve.wait_ge(q["vr_put"], n + 1)
                    src = (tok[0], tok[1], key[0], key[1])[b][0:PR, 0:NC * D].rearrange("p (c d) -> p c d", d=HG * HD)
                    nc.vector.tensor_tensor(vbd[:, L, b].rearrange("p c (g d) -> p (c g) d", g=G), src, vm, ALU.mult).then_inc(q["v_set"], 1)

            def extra_mask():
                dve.wait_ge(q["mask_in"], 32)
                dve.wait_ge(q["krow_set"], B)
                row = kextra[96:97, :].rearrange("p (b j h) -> p b j h", b=B, h=HG)
                for hh_ in range(HG):
                    ins = nc.vector.tensor_scalar(row[:, :, 0:M, hh_], cmask[96:97, :, 0:M], -1.0, -NEG, ALU.add, ALU.mult)
                ins.then_inc(q["extra_ready"], 1)

            def quant_prep():
                dve.wait_ge(q["wffn_in"], 80)
                link(nc.vector.memset(wmx[:, :], 1.0))
                for j, w in ((0, wg0), (3, wu0)):
                    nc.vector.tensor_reduce(wmx[:, j:j + 2], w[:, 0:2, :], AX.X, ALU.max, apply_absolute_value=True)
                    nc.vector.tensor_reduce(wmx[0:IT[2], j + 2:j + 3], w[0:IT[2], 2, :], AX.X, ALU.max, apply_absolute_value=True)
                link(nc.vector.tensor_reduce(wmx[:, 6:7], wd0[:, :], AX.X, ALU.max, apply_absolute_value=True))
                link(nc.vector.tensor_scalar(wmx[:, :], wmx[:, :], 1.0 / QMAX, None, ALU.mult))
                link(nc.vector.reciprocal(rwm[:, :], wmx[:, :]))
                for j, w in ((0, wg0), (3, wu0)):
                    for t in range(3):
                        ins = nc.vector.tensor_scalar(w[0:IT[t], t, :], w[0:IT[t], t, :], rwm[0:IT[t], j + t:j + t + 1], MAGIC, ALU.mult, ALU.add)
                ins = nc.vector.tensor_scalar(wd0[:, :], wd0[:, :], rwm[:, 6:7], MAGIC, ALU.mult, ALU.add)
                ins.then_inc(q["wq_rounded"], 1)
                nc.vector.tensor_scalar(diag[:, :], ident[:, :], wmx[:, 6:7], None, ALU.mult).then_inc(q["sd_diag"], 1)
                dve.wait_ge(q["csc_ready"], 1)
                link(nc.vector.tensor_scalar(eclip[:, :], eclip[:, :], 1.0, None, ALU.add))
                link(nc.vector.reciprocal(csc[:, :], eclip[:, :]))
                link(nc.vector.tensor_scalar(csc[:, :], csc[:, :], 1.0 / QMAX, None, ALU.mult))
                dve.wait_ge(q["sd_put"], 1)
                nc.vector.tensor_copy(sdrow[:, :], key[1][:, 0:D]).then_inc(q["sd_copied"], 1)

            def attention(L):
                for i, k in steps(-2, B):
                    u = B * L + i
                    for c in token_turns(k) if i + 1 in UNITS else ():
                        v = u + 1
                        n = 16 * v + c
                        t, g = divmod(c, G)
                        dve.wait_ge(q["tok_put"], n + 1)
                        if c == 0 and v >= 2:
                            dve.wait_ge(q["mt_put"], v - 1)
                        nc.vector.tensor_reduce(mx[:, v % 2, t, g, 0, :],
                                                tok[n % 2][:, 0:KG].rearrange("p (j h) -> p h j", h=HG), AX.X, ALU.max).then_inc(q["tok_maxed"], 1)
                    if k == AT_Q and i + 2 in UNITS:
                        v = u + 2
                        dve.wait_ge(q["q_hi"], v + 1)
                        if v >= 2:
                            dve.wait_ge(stack_q[v % 2], STQ * (v // 2))
                        nc.vector.scalar_tensor_tensor(qlo[:, v % 2, :], m1[:, :], bq[:, L:L + 1], qhi[:, v % 2, :].bitcast(F32),
                                                       ALU.add, ALU.subtract).then_inc(q["q_lo"], 1)
                    if k == AT_ON and i - 1 in UNITS:
                        dve.wait_ge(q["on_put"], u)
                        link(nc.vector.reciprocal(rden[:, :, :], m1[:, :].rearrange("p (t h d) -> p t h d", t=NT, h=H)[:, :, :, 0]))
                        if u >= 2:
                            dve.wait_ge(q["ot_put"], u - 1)
                        nc.vector.tensor_tensor(on[:, :, :].rearrange("p t (h d) -> p (t h) d", h=H), m0[:, :].rearrange("p (n d) -> p n d", d=HD),
                                                rden[:, :, :].rearrange("p t h -> p (t h)").unsqueeze(2).broadcast_to([128, NT * H, HD]),
                                                ALU.mult).then_inc(q["o_normed"], 1)
                    if k == AT_WO and i - 1 in UNITS:
                        b = i - 1
                        dve.wait_ge(q["att_put"], u)
                        if L == 0:
                            dve.wait_ge(q["xb_set"], NT * (b + 1))
                        nc.vector.tensor_tensor(x[:, NT * b:NT * b + NT, :], m1[:, :].rearrange("p (t d) -> p t d", t=NT),
                                                x[:, NT * b:NT * b + NT, :], ALU.add).then_inc(q["x_attended"], 1)
                        dve.wait_ge(q["x_attended"], u)
                        ln_stats(B * (2 * L + 1) + b)
                    if k == AT_LN and i - 1 in UNITS:
                        n = B * (2 * L + 1) + i - 1
                        ln_apply(n)
                        if L == 0:
                            dve.wait_ge(q["xn_ready"], n + 1)
                            b = n % B
                            nc.vector.tensor_reduce(axb[:, 0, b:b + 1], xn[:, NT * b:NT * b + NT, :], AX.XY, ALU.max, apply_absolute_value=True)
                    if k == AT_MAX and i + 1 in UNITS:
                        v = u + 1
                        dve.wait_ge(q["tok_maxed"], 16 * (v + 1))
                        nc.vector.tensor_copy(mx[:, v % 2, :, :, 1, :].rearrange("p t g h -> p (t g) h"),
                                              mx[:, v % 2, :, :, 0, :].rearrange("p t g h -> p (t g) h")).then_inc(q["mx_doubled"], 1)
                        dve.wait_ge(q["mt_hi"], v + 1)
                        if v >= 2:
                            dve.wait_ge(stack_m[v % 2], STM * (v // 2))
                        nc.vector.scalar_tensor_tensor(mthl[:, v % 2, :], mthi[:, :].bitcast(F32), mpart, m0[0:2 * H, :],
                                                       ALU.mult, ALU.add).then_inc(q["mt_split"], 1)
                    if L == 0 and i == -1 and k == 15:
                        quant_prep()
                        extra_mask()
                        key_split(1)
                        v_blocks(1)

            def whole_max(j):
                dve.wait_ge(q["const_set"], 1)
                link(nc.vector.memset(gm1[0:1, j:j + 1], 0.0))
                nc.vector.tensor_reduce(axm[:, j:j + 1], axb[:, j, :], AX.X, ALU.max).then_inc(q["part_max"], 1)
                dve.wait_ge(q["row_put"], j + 1)
                nc.vector.tensor_reduce(gm1[0:1, j:j + 1], m1[0:1, 0:128], AX.X, ALU.max).then_inc(q["row_max"], 1)
                dve.wait_ge(q["bc_put"], j + 1)
                link(nc.vector.tensor_scalar(qs[:, j:j + 1], m1[:, 256:257], csc[:, j:j + 1], None, ALU.mult))
                link(nc.vector.reciprocal(rqs[:, j:j + 1], qs[:, j:j + 1]))

            for b in range(B):
                dve.wait_ge(x_in[b], 16)
                ln_stats(b)
                if b == 0:
                    ln_apply(0)
                    key_split(0)
            for b in range(1, B):
                ln_apply(b)
            v_blocks(0)
            attention(0)
            if STOP > 1:
                whole_max(0)
                nc.vector.memset(h0[96:128, :, 2, :], 0.0)
                for j in range(2):
                    nc.vector.tensor_scalar(gus[:, 3 * j:3 * j + 2], wmx[:, 3 * j:3 * j + 2], qs[:, 0:1], None, ALU.mult)
                    nc.vector.tensor_scalar(gus[0:IT[2], 3 * j + 2:3 * j + 3], wmx[0:IT[2], 3 * j + 2:3 * j + 3], qs[0:IT[2], 0:1], None, ALU.mult)
                for b in range(B):
                    v = xn[:, NT * b:NT * b + NT, :]
                    link(nc.vector.tensor_scalar(v, v, rqs[:, 0:1], QMAX, ALU.mult, ALU.min))
                    nc.vector.tensor_scalar(v, v, -QMAX - 1.0, MAGIC, ALU.max, ALU.add).then_inc(q["xq_ready"], 1)
                for n in range(3 * B):
                    b, i3 = divmod(n, 3)
                    w = IT[i3]
                    dve.wait_ge(q["silu_ready"], n + 1)
                    dve.wait_ge(q["u_put"], n + 1)
                    nc.vector.scalar_tensor_tensor(h0[0:w, b, i3, :], key[n % 2][0:w, :], gus[0:w, 3 + i3:4 + i3],
                                                   sg[0:w, n % 2, :], ALU.mult, ALU.mult).then_inc(q["h_ready"], 1)
                    if i3 == 2:
                        dve.wait_ge(q["h_ready"], n + 1)
                        link(nc.vector.tensor_reduce(axb[:, 1, b:b + 1], h0[:, b, :, :], AX.XY, ALU.max, apply_absolute_value=True))
                whole_max(1)
                for b in range(B):
                    v = h0[:, b, :, :]
                    link(nc.vector.tensor_scalar(v, v, rqs[:, 1:2], QMAX, ALU.mult, ALU.min))
                    nc.vector.tensor_scalar(v, v, -QMAX - 1.0, MAGIC, ALU.max, ALU.add).then_inc(q["hq_f"], 1)
                    if b == 0:
                        link(nc.vector.tensor_scalar(sdrow[:, :], sdrow[:, :], qs[:, 1:2], None, ALU.mult))
                for b in range(B):
                    dve.wait_ge(q["d_put"], b + 1)
                    link(nc.vector.tensor_tensor(dtmp[:, b % 2, :].rearrange("p (t d) -> p t d", t=NT),
                                                 (m0, m1)[b % 2][:, :].rearrange("p (t d) -> p t d", t=NT),
                                                 sdrow[:, :].unsqueeze(1).broadcast_to([128, NT, D]), ALU.mult))
                    v = x[:, NT * b:NT * b + NT, :]
                    nc.vector.tensor_tensor(v, v, dtmp[:, b % 2, :].rearrange("p (t d) -> p t d", t=NT), ALU.add).then_inc(q["x_ffn"], 1)
                    dve.wait_ge(q["x_ffn"], b + 1)
                    ln_stats(2 * B + b)
                    ln_apply(2 * B + b)
            if STOP > 2:
                attention(1)
            if STOP > 3:
                dve.wait_ge(q["gate_in"], 80)
                link(nc.vector.tensor_copy(gwh[:, :], gwf[:, :]))
                nc.vector.tensor_tensor(gwl[:, :], gwf[:, :], gwh[:, :].bitcast(F32), ALU.subtract)
                nc.vector.tensor_reduce(b2s[:, :], b2[:, :], AX.X, ALU.add).then_inc(q["b2_summed"], 1)

                def x_lo(b):
                    dve.wait_ge(q["x1_hi"], b + 1)
                    if b >= 2:
                        dve.wait_ge(q["w1_put"], NH * (b - 1))
                    nc.vector.tensor_tensor(xl1[:, b % 2, :], m0[:, :], xh1[:, b % 2, :].bitcast(F32), ALU.subtract).then_inc(q["x1_lo"], 1)

                def bc(ap):
                    return ap.unsqueeze(2).broadcast_to([128, NT, E])

                def gate_a(b):
                    dve.wait_ge(q["lg_put"], b + 1)
                    if b >= 1:
                        dve.wait_ge(q["lg_e"], b)
                    link(nc.vector.tensor_tensor(lg[:, :, :], m1[:, 0:NT * E].rearrange("p (t e) -> p t e", t=NT),
                                                 gb[:, :].unsqueeze(1).broadcast_to([128, NT, E]), ALU.add))
                    link(nc.vector.tensor_tensor(lq[:, :, :], lg[:, :, :], lg[:, :, :], ALU.mult))
                    nc.vector.tensor_reduce(s4[:, 0, :], lq[:, :, :], AX.X, ALU.add).then_inc(q["lg_ms"], 1)

                def gate_b(b):
                    dve.wait_ge(q["lg_r"], b + 1)
                    link(nc.vector.tensor_tensor(lg[:, :, :], lg[:, :, :], bc(s4[:, 2, :]), ALU.mult))
                    link(nc.vector.tensor_tensor(lg[:, :, :], lg[:, :, :], rw[:, :].unsqueeze(1).broadcast_to([128, NT, E]), ALU.mult))
                    link(nc.vector.tensor_scalar(lg[:, :, :], lg[:, :, :], 2.0, None, ALU.mult))
                    link(nc.vector.tensor_reduce(s4[:, 3, :], lg[:, :, :], AX.X, ALU.max))
                    nc.vector.tensor_tensor(lg[:, :, :], lg[:, :, :], bc(s4[:, 3, :]), ALU.subtract).then_inc(q["lg_d"], 1)

                def gate_c(b):
                    dve.wait_ge(q["lg_e"], b + 1)
                    link(nc.vector.tensor_reduce(s4[:, 4, :], lq[:, :, :], AX.X, ALU.add))
                    link(nc.vector.reciprocal(s4[:, 4, :], s4[:, 4, :]))
                    link(nc.vector.tensor_scalar(s4[:, 3, :], s4[:, 4, :], 1e-6, None, ALU.add))
                    link(nc.vector.reciprocal(s4[:, 3, :], s4[:, 3, :]))
                    link(nc.vector.tensor_tensor(ng[:, b % 2, :], s4[:, 4, :], s4[:, 3, :], ALU.mult))

                x_lo(0)
                for n in range(NH * B + 6):
                    if n < NH * B:
                        dve.wait_ge(q["gelu_ready"], n + 1)
                        if n >= 3:
                            dve.wait_ge(q["w2_done"], n - 2)
                        nc.vector.tensor_copy(hh[:, n % 3, :], hf[:, n % 3, :]).then_inc(q["h_split"], 1)
                        dve.wait_ge(q["h_split"], 2 * n + 1)
                        nc.vector.tensor_tensor(hl[:, n % 3, :], hf[:, n % 3, :], hh[:, n % 3, :].bitcast(F32), ALU.subtract).then_inc(q["h_split"], 1)
                    b = n // NH
                    if n % NH == 8 and b + 1 < B:
                        x_lo(b + 1)
                    if n % NH == 10 and b < B:
                        gate_a(b)
                    if n % NH == 12 and b < B:
                        gate_b(b)
                    if n % NH == 14 and b < B:
                        gate_c(b)
                    if n % NH == 5 and b >= 1:
                        v = b - 1
                        dve.wait_ge(q["yT_put"], v + 1)
                        for t in range(NT):
                            ins = nc.vector.scalar_tensor_tensor(xn[:, NT * v + t, :], m1[:, 128 * t:128 * t + 128],
                                                                 ng[:, v % 2, t:t + 1], x[:, NT * v + t, :], ALU.mult, ALU.add)
                        ins.then_inc(q["y_done"], 1)
            else:
                for b in range(B):
                    nc.vector.tensor_copy(xn[:, NT * b:NT * b + NT, :], x[:, NT * b:NT * b + NT, :]).then_inc(q["y_done"], 1)

        @block.tensor
        def _(pe):
            mm = nc.tensor.matmul

            def keys_values(L):
                if L == 0:
                    pe.wait_ge(q["ctx_in"], 16)
                    pe.wait_ge(q["wkv_in"], 16)
                    pe.wait_ge(q["ctxr_ready"], 1)
                else:
                    pe.wait_ge(q["wqT_copied"], 4)
                    pe.wait_ge(q["mt_split"], 1)
                    pe.wait_ge(q["tok_maxed"], 16)
                    pe.wait_ge(q["sd_copied"], 1)
                mm(m0[:, 0:B * MP], wk[:, L, :], ctxt[:, :], start=True, stop=True).then_inc(q["kt_put"], 1)
                for b in range(B):
                    if L == 1 and b == 3:
                        pe.wait_ge(q["kt_put"], 2)
                    bank = (tok[0], tok[1], key[0], key[1])[b]
                    for c in range(NC):
                        lo = b * MP + c * JC
                        ins = mm(bank[0:PR, D * c:D * c + D], ctxr[:, lo:lo + JC, :].rearrange("p j h -> p (j h)"), wv[:, L, :], start=True, stop=True)
                    ins.then_inc(q["vr_put"], 1)

            def quant_prep():
                pe.wait_ge(q["wq_rounded"], 1)
                pe.wait_ge(q["tok_maxed"], 16)
                for n, w in enumerate((wg0, wu0)):
                    for t in range(3):
                        ins = nc.tensor.transpose(tok[n][:, 128 * t:128 * t + IT[t]], w[0:IT[t], t, :], ident[0:IT[t], 0:IT[t]])
                    ins.then_inc(q["wqT_put"], 1)
                for t in range(3):
                    ins = nc.tensor.transpose(key[0][0:IT[t], 128 * t:128 * t + 128], wd0[:, 128 * t:128 * t + IT[t]], ident[:, :])
                ins.then_inc(q["wqT_put"], 1)
                pe.wait_ge(q["sd_diag"], 1)
                pe.wait_ge(q["const_set"], 1)
                mm(key[1][:, 0:D], ones[:, :], diag[:, :], start=True, stop=True).then_inc(q["sd_put"], 1)

            def attention(L):
                for i, k in steps(-2, B):
                    u = B * L + i
                    if k == AT_DEN and i - 1 in UNITS:
                        probs_v(L, i - 1, 2, 1)
                    if k == AT_XT and i + 2 in UNITS:
                        v = u + 2
                        pe.wait_ge(q["xn_ready"], 2 * B * L + i + 3)
                        m0_free()
                        if v == 0:
                            pe.wait_ge(q["consts_in"], 16)
                            pe.wait_ge(q["k_split"], 1)
                        for t in range(NT):
                            ins = nc.tensor.transpose(m0[:, 128 * t:128 * t + 128], xn[:, NT * (i + 2) + t, :], ident[:, :])
                        ins.then_inc(q["xt_put"], 1)
                        n_xt[0] += 1
                    for c in token_turns(k) if i + 1 in UNITS else ():
                        v = u + 1
                        s, n = v % 3, 16 * v + c
                        t, g = divmod(c, G)
                        if c == 0:
                            pe.wait_ge(stack_q[v % 2], STQ * (v // 2 + 1))
                            if i + 1 == 0:
                                pe.wait_ge(q["kst_in"], 192 * (L + 1))
                                pe.wait_ge(q["krow_set"], B * (L + 1))
                                pe.wait_ge(q["const_set"], 1)
                                pe.wait_ge(q["v_set"], B * (L + 1))
                        if n >= 2:
                            pe.wait_ge(q["tok_maxed"], n - 1)
                        mm(tok[n % 2][:, 0:KG], qst[0:MASKROW + 1, s, g, 128 * t:128 * t + 128], kst[0:MASKROW + 1, i + 1, g, :],
                           start=True, stop=True).then_inc(q["tok_put"], 1)
                    if i in UNITS and LAG <= k < LAG + 12:
                        n = 12 * u + k - LAG
                        c, g = divmod(k - LAG, G)
                        if k == LAG:
                            pe.wait_ge(stack_m[u % 2], STM * (u // 2 + 1))
                        if n >= 2:
                            pe.wait_ge(q["p_ready"], n - 1)
                        mm(key[n % 2][0:PR, :], kst[0:KROWS, i, g, PR * c:PR * c + PR], qst[0:KROWS, u % 3, g, :],
                           start=True, stop=True).then_inc(q["key_put"], 1)
                    if k in PV and i in UNITS:
                        probs_v(L, i, *PV[k])
                    if k == AT_Q and i + 2 in UNITS:
                        v = u + 2
                        pe.wait_ge(q["xt_copied"], v + 1)
                        pe.wait_ge(q["wqo_in"], 16)
                        m1_free()
                        mm(m1[:, :], wq[:, L, :], xt[:, v % 2, :], start=True, stop=True).then_inc(q["q_put"], 1)
                        n_q[0] += 1
                    if k == AT_ON and i - 1 in UNITS:
                        pe.wait_ge(q["o_copied"], u)
                        m0_free()
                        for t in range(NT):
                            nc.tensor.transpose(m0[:, 128 * t:128 * t + 128], ov[:, 128 * t:128 * t + 128], ident[:, :])
                        m1_free()
                        for t in range(NT):
                            ins = nc.tensor.transpose(m1[:, 128 * t:128 * t + 128], od[:, 128 * t:128 * t + 128], ident[:, :])
                        ins.then_inc(q["on_put"], 1)
                        n_on[0] += 1
                    if k == AT_OT and i - 1 in UNITS:
                        m0_free()
                        for t in range(NT):
                            ins = nc.tensor.transpose(m0[:, 128 * t:128 * t + 128], on[:, t, :], ident[:, :])
                        ins.then_inc(q["ot_put"], 1)
                        n_ot[0] += 1
                    if k == AT_WO and i - 1 in UNITS:
                        pe.wait_ge(q["ot_copied"], u)
                        m1_free()
                        for t in range(NT):
                            ins = mm(m1[:, 128 * t:128 * t + 128], ot[:, 128 * t:128 * t + 128], wo[:, L, :], start=True, stop=True)
                        ins.then_inc(q["att_put"], 1)
                        n_wo[0] += 1
                    if k == AT_MAX and i + 1 in UNITS:
                        v = u + 1
                        pe.wait_ge(q["mx_doubled"], v + 1)
                        m0_free()
                        for t in range(NT):
                            both = mx[:, v % 2, t].rearrange("p g s h -> p (g s h)")
                            ins = nc.tensor.transpose(m0[0:2 * H, 128 * t:128 * t + 128], both, ident[:, :])
                        ins.then_inc(q["mt_put"], 1)
                        n_mt[0] += 1
                    if L == 0 and i == -1 and k == 15:
                        quant_prep()
                        keys_values(1)
                        pe.wait_ge(q["k_split"], 2)
                        pe.wait_ge(q["v_set"], 2 * B)

            def probs_v(L, b, c, den):
                u = B * L + b
                if den == 0:
                    pe.wait_ge(q["p_ready"], 12 * u + G * (c + 1))
                    if c == 0 and u >= 1:
                        pe.wait_ge(q["o_copied"], u)
                for g in range(G):
                    w = vmask if den else vbd[:, L, b, c, 32 * g:32 * g + 32]
                    ins = mm(acc[den][32 * g:32 * g + 32, :], w, p[:, G * c + g, :], start=(c == 0), stop=(c == NC - 1))
                if den:
                    ins.then_inc(q["pv_put"], 1)

            n_on, n_ot, n_xt, n_mt, n_wo, n_q = [0], [0], [0], [0], [0], [0]

            def m0_free():
                for count, name in ((n_on, "o_normed"), (n_ot, "ot_copied"), (n_xt, "xt_copied"), (n_mt, "mt_split")):
                    if count[0]:
                        pe.wait_ge(q[name], count[0])

            def m1_free():
                for count, name in ((n_on, "o_normed"), (n_wo, "x_attended"), (n_q, "q_lo")):
                    if count[0]:
                        pe.wait_ge(q[name], count[0])

            def whole_max(j):
                pe.wait_ge(q["part_max"], j + 1)
                mm(m1[0:1, 0:128], axm[:, j:j + 1], ident[:, :], start=True, stop=True).then_inc(q["row_put"], 1)
                pe.wait_ge(q["row_max"], j + 1)
                mm(m1[:, 256:257], ones[0:1, :], gm1[0:1, j:j + 1], start=True, stop=True).then_inc(q["bc_put"], 1)

            keys_values(0)
            attention(0)
            if STOP > 1:
                whole_max(0)
                for b in range(B):
                    pe.wait_ge(q["xq_ready"], b + 1)
                    if b >= 2:
                        pe.wait_ge(q["xqt_copied"], b - 1)
                    for t in range(NT):
                        ins = nc.tensor.transpose((m0, m1)[b % 2][:, 128 * t:128 * t + 128], xn[:, NT * b + t, :], ident[:, :])
                    ins.then_inc(q["xqt_put"], 1)
                for n in range(3 * B):
                    b, i3 = divmod(n, 3)
                    w, lo = IT[i3], 128 * i3
                    pe.wait_ge(q["xqt_copied"], b + 1)
                    if n >= 2:
                        pe.wait_ge(q["silu_ready"], n - 1)
                    mm(tok[n % 2][0:w, :], wgT[:, lo:lo + w], xqt[:, b, :], start=True, stop=True).then_inc(q["g_put"], 1)
                    if n >= 2:
                        pe.wait_ge(q["h_ready"], n - 1)
                    mm(key[n % 2][0:w, :], wuT[:, lo:lo + w], xqt[:, b, :], start=True, stop=True).then_inc(q["u_put"], 1)
                whole_max(1)
                for b in range(B):
                    pe.wait_ge(q["hq_ready"], b + 1)
                    if b >= 2:
                        pe.wait_ge(q["x_ffn"], b - 1)
                    for t in range(NT):
                        for i3 in range(3):
                            w = IT[i3]
                            ins = mm((m0, m1)[b % 2][:, 128 * t:128 * t + 128], hq[0:w, b, i3, 128 * t:128 * t + 128], wdT[0:w, i3, :],
                                     start=(i3 == 0), stop=(i3 == 2))
                    ins.then_inc(q["d_put"], 1)
            if STOP > 2:
                pe.wait_ge(q["x_ffn"], B)
                attention(1)
            if STOP > 3:
                ring = tok + key

                def x_transposed(b):
                    pe.wait_ge(q["xn_ready"], 3 * B + b + 1)
                    if b == 0:
                        pe.wait_ge(q["ot_copied"], 2 * B)
                    else:
                        pe.wait_ge(q["x1_lo"], b)
                    for t in range(NT):
                        ins = nc.tensor.transpose(m0[:, 128 * t:128 * t + 128], xn[:, NT * b + t, :], ident[:, :])
                    ins.then_inc(q["xt1_put"], 1)

                def logits(b):
                    pe.wait_ge(q["x1_lo"], b + 1)
                    if b == 0:
                        pe.wait_ge(q["b2_summed"], 1)
                        pe.wait_ge(q["x_attended"], 2 * B)
                    if b >= 2:
                        pe.wait_ge(q["y_done"], b - 1)
                    for t in range(NT):
                        tt = slice(128 * t, 128 * t + 128)
                        pairs = [(xh, gw_) for xh in (xh1, xl1) for gw_ in (gwh, gwl)]
                        for j, (xs, gs) in enumerate(pairs):
                            ins = mm(m1[:, E * t:E * t + E], xs[:, b % 2, tt], gs[:, :], start=(j == 0), stop=(j == 3))
                    ins.then_inc(q["lg_put"], 1)

                x_transposed(0)
                logits(0)
                pe.wait_ge(q["w1_split"], 1)
                pe.wait_ge(q["w2_split"], 1)
                for n in range(NH * B + 5):
                    b, j = divmod(n, NH)
                    if n < NH * B:
                        w = slice(128 * j, 128 * j + 128)
                        bank = ring[n % 4]
                        if n >= 4:
                            pe.wait_ge(q["gelu_ready"], n - 3)
                        if j == 0:
                            pe.wait_ge(q["x1_lo"], b + 1)
                        mm(bank[:, :], w1l[:, w], xh1[:, b % 2, :], start=True, stop=False)
                        mm(bank[:, :], w1h[:, w], xl1[:, b % 2, :], start=False, stop=False)
                        mm(bank[:, :], w1h[:, w], xh1[:, b % 2, :], start=False, stop=True).then_inc(q["w1_put"], 1)
                    m = n - 2
                    if 0 <= m < NH * B:
                        bm, jm = divmod(m, NH)
                        w = slice(128 * jm, 128 * jm + 128)
                        pe.wait_ge(q["h_split"], 2 * m + 2)
                        if jm == 0 and bm >= 2:
                            pe.wait_ge(q["yt_copied"], bm - 1)
                        mm(acc[bm % 2][:, :], w2l[:, w], hh[:, m % 3, :], start=(jm == 0), stop=False)
                        mm(acc[bm % 2][:, :], w2h[:, w], hl[:, m % 3, :], start=False, stop=False)
                        mm(acc[bm % 2][:, :], w2h[:, w], hh[:, m % 3, :], start=False, stop=(jm == NH - 1)).then_inc(q["w2_done"], 1)
                    if j == 8 and b + 1 < B:
                        x_transposed(b + 1)
                    if j == 4 and b >= 1:
                        v = b - 1
                        pe.wait_ge(q["yt_copied"], v + 1)
                        pe.wait_ge(q["lg_ms"], v + 1)
                        for t in range(NT):
                            ins = nc.tensor.transpose(m1[:, 128 * t:128 * t + 128], yt[:, 128 * t:128 * t + 128], ident[:, :])
                        ins.then_inc(q["yT_put"], 1)
                    if j == 9 and 1 <= b < B:
                        pe.wait_ge(q["y_done"], b)
                        logits(b)


def shape_constants():
    cst = np.zeros((128, 133 + HG * HD), np.float32)
    cst[:, 0:128] = np.eye(128)
    d = np.arange(128)
    cst[:, 128:132] = (d // HD % HG)[:, None] == np.arange(HG)[None]
    cst[0:2 * H, 132] = -(np.arange(2 * H) // HG % 2)
    cst[0:PR, 133:] = (np.arange(PR) % HG)[:, None] == (np.arange(HG * HD) // HD)[None]
    rows = np.zeros((KROWS - 96, B, MP, HG), np.float32)
    rows[0, :, M:, :] = NEG
    for h in range(HG):
        rows[MHI - 96 + h, :, :, h] = -1.0
        rows[MLO - 96 + h, :, :, h] = -1.0
    return cst, rows.reshape(KROWS - 96, B * KG)


def kernel(**inputs):
    import concourse.bacc as _bacc
    from concourse.bass_utils import run_bass_kernel_spmd as _run

    v = {k: np.asarray(w) for k, w in inputs.items()}
    cst, rows = shape_constants()
    kv = v["L0_xattn_Wkv"].reshape(H, 2, HD, C)
    bkv = v["L0_xattn_bkv"].reshape(H, 2, HD)
    zero = np.zeros((1, D), np.float32)
    ctx = np.zeros((C + 1, B, MP), np.float32)
    ctx[C] = 1.0
    ctx[0:C, :, 0:M] = v["ctx_768"].transpose(2, 0, 1)
    arrays = {
        "x": v["x"],
        "cst": cst, "krows": rows,
        "ctxT": ctx.reshape(C + 1, B * MP),
        "mask": v["mask_BxS2_bf1"].view(np.uint8),
        "wkv": np.stack([np.concatenate([kv[:, 0].reshape(D, C).T, bkv[:, 0].reshape(1, D)]),
                         np.concatenate([v["L1_xattn_Wk"], zero]),
                         np.concatenate([kv[:, 1].reshape(D, C).T, bkv[:, 1].reshape(1, D)]),
                         np.concatenate([v["L1_xattn_Wv"], zero])], 1),
        "wqo": np.stack([v["L0_xattn_Wq"].T, v["L1_xattn_Wq"], v["L0_xattn_Wo"].T, v["L1_xattn_Wo"]], 1),
        "bq": v["L0_xattn_bq"].reshape(D, 1),
        "bo": v["L0_xattn_bo"],
        "clip": np.concatenate([v["L0_ffn_clip_x"], v["L0_ffn_clip_down"]]),
        "w_gate": v["L0_ffn_w_gate"], "w_up": v["L0_ffn_w_up"], "w_down": v["L0_ffn_w_down"],
        "gate_wT": v["L1_ffn_gate_w"].T, "gate_b": v["L1_ffn_gate_b"], "rms_w": v["L1_ffn_rms_w"],
        "w1": v["L1_ffn_w1"], "b1": v["L1_ffn_b1"].reshape(NH, 128).T,
        "w2": v["L1_ffn_w2"], "b2": v["L1_ffn_b2"].T,
    }
    nc = _bacc.Bacc("TRN2", target_bir_lowering=False, num_devices=1)
    feeds, aps = {}, {}
    for name, w in arrays.items():
        w = np.ascontiguousarray(w)
        feeds["in_" + name] = w
        aps[name] = nc.dram_tensor("in_" + name, w.shape, mybir.dt.from_np(w.dtype), kind="ExternalInput").ap()
    out = nc.dram_tensor("out_0", (B, S, D), F32, kind="ExternalOutput").ap()
    build(nc, aps, out)
    r = _run(nc, [feeds], core_ids=[0])
    return r.results[0]["out_0"]
```

```python
from contextlib import ExitStack

import numpy as np

import concourse.bass as bass
from concourse import mybir

F32 = mybir.dt.float32
F32R = mybir.dt.float32r
BF16 = mybir.dt.bfloat16
U8 = mybir.dt.uint8
ALU = mybir.AluOpType
ACT = mybir.ActivationFunctionType
AX = mybir.AxisListType

B, S, D = 4, 512, 128
NT = S // 128
M, MP = 77, 78
C = 96
H, HD = 16, 8
G, HG = 4, 4
NC = 3
JC = MP // NC
PR = JC * HG
KG = MP * HG
MASKROW, MHI, MLO, KROWS = 96, 97, 101, 105
I0 = 352
IT = [128, 128, 96]
E, HE = 8, 256
NH = E * HE // 128
STQ, STM = 16 * 3, 16
SCALE = float(HD) ** -0.5
NEG = -(2.0 ** 127)
MAGIC = 1.5 * 2.0 ** 23
QMAX = 127.0
HR, HLAG = 6, 4
LN_EPS = 1e-5
EPS32 = float(np.finfo(np.float32).eps)


def build(nc, a, out):
    with ExitStack() as ctx:
        def sb(name, shape, dt=F32):
            return ctx.enter_context(nc.sbuf_tensor(name, shape, dt))

        def ps(name):
            return ctx.enter_context(nc.psum_tensor(name, [128, 512], F32))

        def sem(name):
            return ctx.enter_context(nc.semaphore(name))

        x = sb("x", [128, B * NT, D])
        xn = sb("xn", [128, B * NT, D])
        stats = sb("stats", [128, B, NT, 6])
        mv = sb("mv", [128, B, NT, 2])
        veps = sb("veps", [128, B, NT])
        rstd = sb("rstd", [128, B, NT])
        mhalf = sb("mhalf", [128, NT * E])
        ebase = sb("ebase", [128, NT * E])
        cst = sb("cst", [128, 133 + HG * HD])
        ident = cst[:, 0:128]
        unread = sb("unread", [1, 2])
        magic = sb("magic", [128, 1])
        ctxt = sb("ctxt", [C + 1, B * MP])
        wkv = sb("wkv", [C + 1, 4, D])
        wk, wv = wkv[:, 0:2, :], wkv[:, 2:4, :]
        wqo = sb("wqo", [D, 4, D])
        wq, wo = wqo[:, 0:2, :], wqo[:, 2:4, :]
        bq = sb("bq", [D, 2])
        bo = sb("bo_sb", [128, D])
        kmask = cst[:, 128:128 + HG]
        mpart = cst[0:2 * H, 132:133]
        vmask = cst[0:PR, 133:133 + HG * HD]
        cmask = sb("cmask", [128, B, MP], U8)
        khi = sb("khi", [D, B * MP], F32R)
        klo = sb("klo", [D, B * MP], F32R)
        rbuf = sb("rbuf", [128, 2 * B * KG], F32R)
        kbd = rbuf[:, 0:2 * B * KG].rearrange("p (s c h) -> p s c h", s=2, h=HG)
        kextra = sb("kextra", [128, B * KG])
        kst = sb("kst", [128, B, G, KG], F32R)
        vbd = sb("vbd", [PR, 2, B, NC, D])
        qhi = sb("qhi", [128, 2, S], F32R)
        qlo = sb("qlo", [128, 2, S], F32R)
        qst = sb("qst", [128, 3, G, S], F32R)
        hring = qst[:, :, :, :].rearrange("p s g c -> p (s g) c")
        hh, hl = hring[:, 0:HR, :], hring[:, HR:2 * HR, :]
        mx = sb("mx", [128, 2, NT, G, 2, HG])
        mthi = sb("mthi", [2 * H, S], F32R)
        mthl = sb("mthl", [2 * H, 2, S], F32R)
        big = sb("big", [128, G * NC * S])
        p = big[0:PR, :].rearrange("p (n c) -> p n c", n=G * NC)
        h0 = big[:, :].rearrange("p (b n c) -> p b n c", b=B, n=3)
        hf = big[:, 0:HR * S].rearrange("p (n c) -> p n c", n=HR)
        yt = big[:, HR * S:(HR + 1) * S]
        tbuf = sb("tbuf", [128, 6 * S])
        xt = tbuf[:, 0:2 * S].rearrange("p (n c) -> p n c", n=2)
        ov = tbuf[:, 2 * S:3 * S]
        od = tbuf[:, 3 * S:4 * S]
        on = tbuf[:, 4 * S:5 * S].rearrange("p (t d) -> p t d", t=NT)
        ot = tbuf[:, 5 * S:6 * S]
        sg = tbuf[:, 2 * S:6 * S].rearrange("p (n c) -> p n c", n=4)
        hq = tbuf[:, :].bitcast(BF16).rearrange("p (b n c) -> p b n c", b=B, n=3)
        sbuf4 = sb("sbuf4", [128, 2 * S])
        dtmp = sbuf4[:, :].rearrange("p (n c) -> p n c", n=2)
        rden = sb("rden", [128, NT, H])

        wg0 = sb("wg0", [128, 3, D])
        wu0 = sb("wu0", [128, 3, D])
        wd0 = sb("wd0", [D, I0])
        wmx = sb("wmx", [128, 7])
        rwm = sb("rwm", [128, 7])
        wgT = sb("wgT", [D, I0], BF16)
        wuT = sb("wuT", [D, I0], BF16)
        wdT = sb("wdT", [128, 3, D], BF16)
        clip = sb("clip", [128, 2])
        eclip = sb("eclip", [128, 2])
        csc = sb("csc", [128, 2])
        diag = sb("diag", [D, D])
        sdrow = sb("sdrow", [128, D])
        ones = sb("ones", [128, 128])
        axb = sb("axb", [128, 2, B])
        axm = sb("axm", [128, 2])
        gm1 = sb("gm1", [1, 2])
        qs = sb("qs", [128, 2])
        rqs = sb("rqs", [128, 2])
        gus = sb("gus", [128, 6])
        xqt = sb("xqt", [D, B, S], BF16)

        w1f = sb("w1f", [128, E * HE])
        ctxr = w1f[0:C + 1, 0:B * KG].rearrange("p (j h) -> p j h", h=HG)
        kf = w1f[:, B * KG:B * KG + B * MP]
        w1h = sb("w1h", [128, E * HE], F32R)
        w1l = sb("w1l", [128, E * HE], F32R)
        w2h = sb("w2h", [128, NH * D], F32R)
        w2l = sb("w2l", [128, NH * D], F32R)
        b1 = sb("b1", [128, NH])
        b2 = sb("b2", [D, E])
        b2s = sb("b2s", [D, 1])
        gwf = sb("gwf", [D, E])
        gwhl = sb("gwhl", [D, 2, E], F32R)
        gwh, gwl = gwhl[:, 0, :], gwhl[:, 1, :]
        gb = sb("gb", [128, E])
        rw = sb("rw", [128, E])
        xh1, xl1 = qhi, qlo
        lg = sb("lg", [128, NT, E])
        lq = sb("lq", [128, NT, E])
        s4 = sb("s4", [128, 6, NT])
        ng = sb("ng", [128, 2, NT])

        tok = [ps(f"ps_tok{i}") for i in range(2)]
        key = [ps(f"ps_key{i}") for i in range(2)]
        acc = [ps(f"ps_acc{i}") for i in range(2)]
        m0 = ps("ps_m0")
        m1 = ps("ps_m1")

        gate_bank, up_bank = tok + acc, key + [m0, m1]

        x_in = [sem(f"x_in{b}") for b in range(B)]
        s_names = (
            "consts_in bo_in ctx_in wkv_in wqo_in bq_in mask_in wffn_in clip_in w1_in w2_in gate_in "
            "const_set extra_ready ctxr_ready kt_put k_split krow_set vr_put v_set xb_set "
            "var_ready eps_self rstd_ready xn_ready xt_put xt_copied q_put q_hi q_lo "
            "tok_put tok_maxed mt_put mx_doubled mt_hi mt_split key_put p_ready pv_put o_copied on_put o_normed ot_put ot_copied "
            "att_put x_attended dve_self pool_self "
            "wq_rounded wqT_put wqT_copied sd_diag sd_put csc_ready "
            "part_max row_put row_max bc_put nt_put nt_copied ax_ready h_cleared gus_ready xq_ready xq_pool rq_ready xqt_copied g_put u_put silu_ready h_ready "
            "hq_f hq_ready d_put x_ffn w1_split w2_split b2_summed xt1_put x1_hi x1_lo lg_put lg_ms lg_r lg_d lg_e "
            "w1_put gelu_ready h_split w2_done yt_copied yT_put y_done out_done"
        )
        q = {n: sem(n) for n in s_names.split()}
        stack_q = [[sem(f"stack_q{i}_{g}") for g in range(G)] for i in range(2)]
        kst_in = [sem(f"kst_in{g}") for g in range(G)]
        stack_m = [[sem(f"stack_m{i}_{g}") for g in range(G)] for i in range(2)]

        block = ctx.enter_context(nc.Block())
        UNITS = range(B)
        AT = (dict(
            xt=[-32.1],
            q=[-29.6],
            tok=[-15.5 + 0.75 * c for c in range(NT * G)],
            max=[-4],
            key=[2 + j for j in range(NC * G)],
            pv=[7.1, 8.1, 11.4, 12.1, 15.1, 16.1],
            copy=[17.2],
            on=[20.1],
            ot=[21.3],
            wo=[24],
            ln=[26.4],
        ), dict(
            xt=[-32.3],
            q=[-29.3],
            tok=[-15.5 + 0.75 * c for c in range(NT * G)],
            max=[-3.9],
            key=[2 + 0.85 * j for j in range(NC * G)],
            pv=[6.2, 8.1, 11.1, 11.9, 15.1, 16.1],
            copy=[17.2],
            on=[19.7],
            ot=[21.7],
            wo=[23.8],
            ln=[26.8],
        ))
        BESIDE = dict(krow=[-31.4, -27.9, -9.9, 6.1], vr0=[-28.6, -25, -12.2, -10.4], lnstat=[-34.5, -26, -12, 4], lnx0=[-34, -23, -8, 8],
                      nt=[29.8, 46.3, 62.3, 78.3], round=[12, 20, 28], wqt=[46, 48, 51, 53], kt=[55], vr=[56.1, 58, 60.8, 62.1])
        FFN = dict(hround=[-42, -41, -15, -5], down=[-40.1, -31.7, -13.1, -3.1], lnx=[-37.6, -25, -9, 4],
                   gset=[30], x1=[31.1, 48.6], experts=[64.5 + 0.914 * n for n in range(NH)])

        AT_YT, AT_Y, AT_LOG, AT_A, AT_B, AT_C = HLAG + 2, HLAG + 3, 12, 13, 15, 5
        FIRST_LOG, FIRST_A, FIRST_B, FIRST_C = 5, 6, 8, 12

        ACT_LATE = dict(copy=0.4, key=0.2)
        DVE_LATE = dict(on=0.1)

        def order(L, late={}):
            jobs = [(16 * b + t + late.get(job, 0), job, b, part) for b in UNITS for job, times in AT[L].items() for part, t in enumerate(times)]
            jobs += [(t, job, part, 0) for job, times in (FFN if L else BESIDE).items() for part, t in enumerate(times)]
            jobs.sort(key=lambda entry: entry[0])
            return [entry[1:] for entry in jobs]

        @block.sync
        def _(sp):
            for b in range(B):
                sp.dma_start(x[:, NT * b:NT * b + NT, :], a["x"][b].rearrange("(t p) d -> p t d", p=128)).then_inc(x_in[b], 16)
                if b == 0:
                    sp.dma_start(wqo[:, :, :], a["wqo"]).then_inc(q["wqo_in"], 16)
                    sp.dma_start(bq[:, 0:1], a["bq"]).then_inc(q["bq_in"], 16)
                    sp.dma_start(kextra[96:KROWS, :], a["krows"]).then_inc(q["mask_in"], 16)
            sp.dma_start(cmask[:, :, 0:M], a["mask"].partition_broadcast(128)).then_inc(q["mask_in"], 16)
            for w, src in ((wg0, a["w_gate"]), (wu0, a["w_up"])):
                sp.dma_start(w[:, 0:2, :], src[0:256, :].rearrange("(t p) d -> p t d", p=128)).then_inc(q["wffn_in"], 16)
                sp.dma_start(w[0:IT[2], 2, :], src[256:I0, :]).then_inc(q["wffn_in"], 16)
            sp.dma_start(wd0[:, :], a["w_down"]).then_inc(q["wffn_in"], 16)

            sp.dma_start(bo[:, :], a["bo"].partition_broadcast(128)).then_inc(q["bo_in"], 16)
            sp.dma_start(clip[:, :], a["clip"].partition_broadcast(128)).then_inc(q["clip_in"], 16)

            def move(dst, src, done):
                sp.dma_start(dst.bitcast(F32), src.bitcast(F32)).then_inc(done, 16)

            def key_stack(g):
                for r, half in enumerate((0, 0, 1)):
                    sp.dma_start(kst[32 * r:32 * r + 32, :, g, :].bitcast(F32),
                                 kbd[32 * g:32 * g + 32, half, :, :].rearrange("p (b j) h -> p b (j h)", b=B).bitcast(F32)
                                 ).then_inc(kst_in[g], 16)

            for L in range(2):
                sp.wait_ge(q["k_split"], L + 1)
                if L == 1:
                    sp.wait_ge(q["key_put"], 12 * B)
                    for g in range(G):
                        key_stack(g)
                for job, b, part in order(L):
                    u = B * L + b
                    if job == "q":
                        s = u % 3
                        if u == 0:
                            key_stack(0)
                        sp.wait_ge(q["q_hi"], u + 1)
                        if u >= 3:
                            sp.wait_ge(q["key_put"], 12 * (u - 2))
                        for g in range(G):
                            r = slice(32 * g, 32 * g + 32)
                            if u == 0 and g > 0:
                                key_stack(g)
                            move(qst[0:32, s, g, :], qhi[r, u % 2, :], stack_q[u % 2][g])
                            move(qst[64:96, s, g, :], qhi[r, u % 2, :], stack_q[u % 2][g])
                            if g == 0:
                                sp.wait_ge(q["q_lo"], u + 1)
                            move(qst[32:64, s, g, :], qlo[r, u % 2, :], stack_q[u % 2][g])
                    if job == "max":
                        sp.wait_ge(q["mt_split"], u + 1)
                        for g in range(G):
                            move(qst[MHI:KROWS, u % 3, g, :], mthl[8 * g:8 * g + 8, u % 2, :], stack_m[u % 2][g])
            for b in range(B):
                sp.wait_ge(q["y_done"], b + 1)
                sp.dma_start(out[b].rearrange("(t p) d -> p t d", p=128), xn[:, NT * b:NT * b + NT, :]).then_inc(q["out_done"], 16)
            sp.wait_ge(q["out_done"], 16 * B)

        @block.gpsimd
        def _(pool):
            sent = {}

            def done(ins, name):
                sent[name] = sent.get(name, 0) + 1
                ins.then_inc(q[name], 1)
                pool.wait_ge(q[name], sent[name])

            done(nc.gpsimd.memset(mhalf[:, :], -0.5), "pool_self")

            def rstd_of(n):
                b = n % B
                pool.wait_ge(q["var_ready"], n + 1)
                done(nc.gpsimd.tensor_scalar(veps[:, b, :], mv[:, b, :, 1], LN_EPS, None, ALU.add), "eps_self")
                done(nc.gpsimd.tensor_tensor(rstd[:, b, :], veps[:, b, :], mhalf[:, 0:NT], ALU.pow), "rstd_ready")

            rstd_of(0)
            done(nc.gpsimd.memset(bq[:, 1:2], 0.0), "pool_self")
            done(nc.gpsimd.memset(qst[96:128, :, :, :].bitcast(F32), 1.0), "const_set")
            for ap, value in ((ebase[:, :], float(np.e)), (magic[:, :], -MAGIC), (ones[:, :], 1.0), (axb[:, :, :], 0.0)):
                done(nc.gpsimd.memset(ap, value), "const_set")
            for b in range(1, B):
                rstd_of(b)
            pool.dma_start(gwf[:, :], a["gate_wT"]).then_inc(q["gate_in"], 16)
            pool.dma_start(gb[:, :], a["gate_b"].partition_broadcast(128)).then_inc(q["gate_in"], 16)
            pool.dma_start(rw[:, :], a["rms_w"].partition_broadcast(128)).then_inc(q["gate_in"], 16)
            pool.dma_start(b1[:, :], a["b1"]).then_inc(q["gate_in"], 16)
            pool.dma_start(b2[:, :], a["b2"]).then_inc(q["gate_in"], 16)
            pool.wait_ge(q["bo_in"], 16)
            for b in range(B):
                pool.wait_ge(q["xn_ready"], b + 1)
                for t in range(NT):
                    done(nc.gpsimd.tensor_tensor(x[:, NT * b + t, :], x[:, NT * b + t, :], bo[:, :], ALU.add), "xb_set")
            for n in range(B, 2 * B - 1):
                rstd_of(n)
            pool.wait_ge(q["vr_put"], 2 * B)
            pool.wait_ge(q["k_split"], 2)
            pool.dma_start(w1f[:, :].rearrange("d (e h) -> d e h", e=E), a["w1"].rearrange("e d h -> d e h")).then_inc(q["w1_in"], 16)
            rstd_of(2 * B - 1)
            pool.wait_ge(q["pv_put"], 3 * B)
            done(nc.gpsimd.memset(h0[96:128, :, 2, :], 0.0), "h_cleared")

            pool.wait_ge(q["rq_ready"], 1)
            for b in range(2, B):
                v = xn[:, NT * b:NT * b + NT, :]
                pool.wait_ge(q["nt_copied"], b + 1)
                done(nc.gpsimd.tensor_scalar(v, v, rqs[:, 0:1], QMAX, ALU.mult, ALU.min), "pool_self")
                done(nc.gpsimd.tensor_scalar(v, v, -QMAX - 1.0, MAGIC, ALU.max, ALU.add), "xq_pool")
            pool.wait_ge(q["w1_in"], 16)
            done(nc.gpsimd.tensor_copy(w1h[:, :], w1f[:, :]), "pool_self")
            done(nc.gpsimd.tensor_tensor(w1l[:, :], w1f[:, :], w1h[:, :].bitcast(F32), ALU.subtract), "w1_split")
            pool.dma_start(w1f[:, :].rearrange("p (n d) -> p n d", n=NH),
                           a["w2"].rearrange("e (s p) d -> p (e s) d", p=128)).then_inc(q["w2_in"], 16)
            for n in range(2 * B, 3 * B):
                rstd_of(n)
            pool.wait_ge(q["w2_in"], 16)
            done(nc.gpsimd.tensor_copy(w2h[:, :], w1f[:, :]), "pool_self")
            done(nc.gpsimd.tensor_tensor(w2l[:, :], w1f[:, :], w2h[:, :].bitcast(F32), ALU.subtract), "w2_split")
            for n in range(3 * B, 4 * B):
                rstd_of(n)
            for b in range(B):
                pool.wait_ge(q["lg_ms"], b + 1)
                done(nc.gpsimd.tensor_scalar(s4[:, 1, :], s4[:, 0, :], 1.0 / E, EPS32, ALU.mult, ALU.add), "pool_self")
                done(nc.gpsimd.tensor_tensor(s4[:, 2, :], s4[:, 1, :], mhalf[:, 0:NT], ALU.pow), "lg_r")
                pool.wait_ge(q["lg_d"], b + 1)
                done(nc.gpsimd.tensor_tensor(lq[:, :, :], ebase[:, :].rearrange("p (t e) -> p t e", t=NT), lg[:, :, :], ALU.pow), "lg_e")

        @block.scalar
        def _(act):
            act.dma_start(ctxt[:, :], a["ctxT"]).then_inc(q["ctx_in"], 16)
            act.dma_start(wkv[:, :, :], a["wkv"]).then_inc(q["wkv_in"], 16)
            act.dma_start(cst[:, :], a["cst"]).then_inc(q["consts_in"], 16)

            act.wait_ge(q["ctx_in"], 16)
            act.activation(ctxr[:, :, :], ctxt[:, :].unsqueeze(2).broadcast_to([C + 1, B * MP, HG]), ACT.Copy).then_inc(q["ctxr_ready"], 1)
            def key_rows(L, b):
                r = slice(96, KROWS)
                if L == 0:
                    act.wait_ge(q["mask_in"], 32)
                else:
                    act.wait_ge(q["extra_ready"], 1)
                    act.wait_ge(q["key_put"], 12 * B)
                src = kextra[r, b * KG:(b + 1) * KG]
                act.activation(kst[r, b], src.unsqueeze(1).broadcast_to([KROWS - 96, G, KG]), ACT.Copy).then_inc(q["krow_set"], 1)

            def weights_transposed(j):
                if j == 0:
                    act.wait_ge(q["clip_in"], 16)
                    act.activation(eclip[:, :], clip[:, :], ACT.Exp, scale=-1.0).then_inc(q["csc_ready"], 1)
                if j == 3:
                    act.wait_ge(q["sd_put"], 1)
                    act.activation(sdrow[:, :], tok[1][:, 0:D], ACT.Copy).then_inc(q["wqT_copied"], 1)
                    return
                act.wait_ge(q["wqT_put"], j + 1)
                src = tok[j % 2]
                if j < 2:
                    act.activation((wgT, wuT)[j][:, :], src[:, 0:I0], ACT.Identity, bias=magic[:, 0:1]).then_inc(q["wqT_copied"], 1)
                else:
                    act.activation(wdT[:, 0:2, :], src[:, 0:256].rearrange("p (t d) -> p t d", t=2), ACT.Identity, bias=magic[:, 0:1])
                    act.activation(wdT[0:IT[2], 2, :], src[0:IT[2], 256:384], ACT.Identity, bias=magic[0:IT[2], 0:1]).then_inc(q["wqT_copied"], 1)

            def attention(L):
                for job, b, j in order(L, ACT_LATE):
                    u = B * L + b
                    if job == "key":
                        n = 12 * u + j
                        act.wait_ge(q["key_put"], n + 1)
                        if u >= 1:
                            act.wait_ge(q["pv_put"], 3 * (u - 1) + j // G + 1)
                        act.activation(p[:, j, :], key[n % 2][0:PR, :], ACT.Exp, scale=SCALE).then_inc(q["p_ready"], 1)
                    if job == "xt":
                        act.wait_ge(q["xt_put"], u + 1)
                        if u >= 2:
                            act.wait_ge(q["q_put"], u - 1)
                        act.activation(xt[:, u % 2, :], m0[:, :], ACT.Copy).then_inc(q["xt_copied"], 1)
                    if job == "copy":
                        act.wait_ge(q["pv_put"], 3 * (u + 1))
                        if u >= 1:
                            act.wait_ge(q["on_put"], u)
                        act.activation(ov[:, :], acc[0][:, :], ACT.Copy)
                        act.activation(od[:, :], acc[1][:, :], ACT.Copy).then_inc(q["o_copied"], 1)
                    if job == "q":
                        act.wait_ge(q["q_put"], u + 1)
                        if u >= 2:
                            for g in range(G):
                                act.wait_ge(stack_q[u % 2][g], STQ * (u // 2))
                        if u == 0:
                            act.wait_ge(q["bq_in"], 16)
                        if u == B:
                            act.wait_ge(q["const_set"], 5)
                        act.activation(qhi[:, u % 2, :], m1[:, :], ACT.Identity, bias=bq[:, L:L + 1]).then_inc(q["q_hi"], 1)
                    if job == "ot":
                        act.wait_ge(q["ot_put"], u + 1)
                        if u >= 1:
                            act.wait_ge(q["att_put"], u)
                        act.activation(ot[:, :], m0[:, :], ACT.Copy).then_inc(q["ot_copied"], 1)
                    if job == "max":
                        act.wait_ge(q["mt_put"], u + 1)
                        if u >= 1:
                            act.wait_ge(q["mt_split"], u)
                        act.activation(mthi[:, :], m0[0:2 * H, :], ACT.Copy).then_inc(q["mt_hi"], 1)
                    if job == "wqt":
                        weights_transposed(b)
                    if job == "krow":
                        key_rows(0, b)
                    if job == "nt":
                        act.wait_ge(q["nt_put"], b + 1)
                        act.wait_ge(q["ax_ready"], b + 1)
                        act.activation(xn[:, NT * b:NT * b + NT, :].rearrange("p t d -> p (t d)"), m0[:, :], ACT.Copy).then_inc(q["nt_copied"], 1)
                    if job == "hround":
                        act.wait_ge(q["hq_f"], b + 1)
                        act.activation(hq[:, b, :, :], h0[:, b, :, :], ACT.Identity, bias=magic[:, 0:1]).then_inc(q["hq_ready"], 1)
                    if job == "x1":
                        x_hi(b)
                    if job == "experts":
                        expert_step(b)

            def x_hi(b):
                act.wait_ge(q["xt1_put"], b + 1)
                if b < 2:
                    for g in range(G):
                        act.wait_ge(stack_q[b % 2][g], STQ * B)
                else:
                    act.wait_ge(q["w1_put"], NH * (b - 1))
                act.activation(xh1[:, b % 2, :], m0[:, :], ACT.Copy).then_inc(q["x1_hi"], 1)

            def expert_step(n):
                if n < NH * B:
                    act.wait_ge(q["w1_put"], n + 1)
                    if n == 0:
                        act.wait_ge(q["pv_put"], 6 * B)
                    if n >= HR:
                        act.wait_ge(q["h_split"], 2 * (n - HR + 1))
                    act.activation(hf[:, n % HR, :], (tok + key)[n % 4][:, :], ACT.Gelu, bias=b1[:, n % NH:n % NH + 1]).then_inc(q["gelu_ready"], 1)
                if n % NH == 8 and 2 <= n // NH + 1 < B:
                    x_hi(n // NH + 1)
                if n % NH == HLAG + 1 and n >= NH:
                    b = n // NH - 1
                    act.wait_ge(q["w2_done"], NH * (b + 1))
                    if b == 0:
                        act.wait_ge(q["b2_summed"], 1)
                    if b >= 1:
                        act.wait_ge(q["yT_put"], b)
                    act.activation(yt[:, :], acc[b % 2][:, :], ACT.Identity, bias=b2s[:, 0:1]).then_inc(q["yt_copied"], 1)

            attention(0)

            def x_integers(b):
                if b < 2:
                    act.wait_ge(q["xq_ready"], b + 1)
                else:
                    act.wait_ge(q["xq_pool"], b - 1)
                act.activation(xqt[:, b, :], xn[:, NT * b:NT * b + NT, :].rearrange("p t d -> p (t d)"), ACT.Identity, bias=magic[:, 0:1]
                               ).then_inc(q["xqt_copied"], 1)

            act.activation(unread[0:1, 0:1], magic[0:1, 0:1], ACT.Silu)
            x_integers(0)
            act.wait_ge(q["gus_ready"], 1)
            for n in range(3 * B):
                b, i3 = divmod(n, 3)
                w = IT[i3]
                act.wait_ge(q["g_put"], n + 1)
                if n >= 4:
                    act.wait_ge(q["h_ready"], n - 3)
                act.activation(sg[0:w, n % 4, :], gate_bank[n % 4][0:w, :], ACT.Silu, scale=gus[0:w, i3:i3 + 1]).then_inc(q["silu_ready"], 1)
                if n in (0, 3, 6):
                    x_integers(1 + n // 3)
            for b in range(B):
                key_rows(1, b)
            act.wait_ge(q["h_ready"], 3 * B)
            act.activation(unread[0:1, 1:2], magic[0:1, 0:1], ACT.Exp)
            attention(1)
            for n in range(NH, NH * B + HLAG + 2):
                expert_step(n)

        @block.vector
        def _(dve):
            link_n = [0]

            def link(ins):
                link_n[0] += 1
                ins.then_inc(q["dve_self"], 1)
                dve.wait_ge(q["dve_self"], link_n[0])

            def ln_stats(n):
                b = n % B
                for t in range(NT):
                    ins = nc.vector.bn_stats(stats[:, b, t, :], x[:, NT * b + t, :])
                link(ins)
                for t in range(NT):
                    ins = nc.vector.bn_aggr(mv[:, b, t, :], stats[:, b, t, :])
                ins.then_inc(q["var_ready"], 1)

            def ln_apply(n):
                b = n % B
                dve.wait_ge(q["rstd_ready"], n + 1)
                for t in range(NT):
                    ins = nc.vector.tensor_scalar(xn[:, NT * b + t, :], x[:, NT * b + t, :], mv[:, b, t, 0:1],
                                                  rstd[:, b, t:t + 1], ALU.subtract, ALU.mult)
                ins.then_inc(q["xn_ready"], 1)

            def key_split(L):
                dve.wait_ge(q["kt_put"], L + 1)
                if L == 0:
                    dve.wait_ge(q["consts_in"], 16)
                    link(nc.vector.tensor_copy(kf[:, :], key[0][:, 0:B * MP]))
                else:
                    dve.wait_ge(q["mask_in"], 32)
                    link(nc.vector.memset(cmask[:, :, M:MP], 0))
                    for g in range(G):
                        dve.wait_ge(kst_in[g], 48)
                    link(nc.vector.tensor_tensor(kf[:, :], tok[0][:, 0:B * MP], cmask[:, :, :].rearrange("p b j -> p (b j)"), ALU.mult))
                link(nc.vector.tensor_copy(khi[:, :], kf[:, :]))
                link(nc.vector.tensor_tensor(klo[:, :], kf[:, :], khi[:, :].bitcast(F32), ALU.subtract))
                for half, src in enumerate((khi, klo)):
                    for hh_ in range(HG):
                        ins = nc.vector.tensor_scalar(kbd[:, half, :, hh_], src[:, :].bitcast(F32), kmask[:, hh_:hh_ + 1], None, ALU.mult)
                ins.then_inc(q["k_split"], 1)

            def v_blocks(L, b):
                vm = vmask.unsqueeze(1).broadcast_to([PR, NC * G, HG * HD])
                dve.wait_ge(q["vr_put"], B * L + b + 1)
                bank = (acc, tok)[L][b % 2]
                src = bank[0:PR, 0:NC * D].rearrange("p (c d) -> p c d", d=HG * HD)
                nc.vector.tensor_tensor(vbd[:, L, b].rearrange("p c (g d) -> p (c g) d", g=G), src, vm, ALU.mult).then_inc(q["v_set"], 1)

            def extra_mask():
                dve.wait_ge(q["mask_in"], 32)
                dve.wait_ge(q["krow_set"], B)
                row = kextra[96:97, :].rearrange("p (b j h) -> p b j h", b=B, h=HG)
                for hh_ in range(HG):
                    ins = nc.vector.tensor_scalar(row[:, :, 0:M, hh_], cmask[96:97, :, 0:M], -1.0, -NEG, ALU.add, ALU.mult)
                ins.then_inc(q["extra_ready"], 1)

            def weight_scales():
                dve.wait_ge(q["wffn_in"], 80)
                link(nc.vector.memset(wmx[:, :], 1.0))
                for j, w in ((0, wg0), (3, wu0)):
                    nc.vector.tensor_reduce(wmx[:, j:j + 2], w[:, 0:2, :], AX.X, ALU.max, apply_absolute_value=True)
                    nc.vector.tensor_reduce(wmx[0:IT[2], j + 2:j + 3], w[0:IT[2], 2, :], AX.X, ALU.max, apply_absolute_value=True)
                link(nc.vector.tensor_reduce(wmx[:, 6:7], wd0[:, :], AX.X, ALU.max, apply_absolute_value=True))
                link(nc.vector.tensor_scalar(wmx[:, :], wmx[:, :], 1.0 / QMAX, None, ALU.mult))
                link(nc.vector.reciprocal(rwm[:, :], wmx[:, :]))

            def weights_rounded():
                for j, w in ((0, wg0), (3, wu0)):
                    for t in range(3):
                        ins = nc.vector.tensor_scalar(w[0:IT[t], t, :], w[0:IT[t], t, :], rwm[0:IT[t], j + t:j + t + 1], MAGIC, ALU.mult, ALU.add)
                ins = nc.vector.tensor_scalar(wd0[:, :], wd0[:, :], rwm[:, 6:7], MAGIC, ALU.mult, ALU.add)
                ins.then_inc(q["wq_rounded"], 1)
                nc.vector.tensor_scalar(diag[:, :], ident[:, :], wmx[:, 6:7], None, ALU.mult).then_inc(q["sd_diag"], 1)

            def clip_scales():
                dve.wait_ge(q["csc_ready"], 1)
                link(nc.vector.tensor_scalar(eclip[:, :], eclip[:, :], 1.0, None, ALU.add))
                link(nc.vector.reciprocal(csc[:, :], eclip[:, :]))
                link(nc.vector.tensor_scalar(csc[:, :], csc[:, :], 1.0 / QMAX, None, ALU.mult))

            def attention(L):
                for job, b, j in order(L, DVE_LATE):
                    u = B * L + b
                    if job == "tok":
                        n = 16 * u + j
                        g, t = divmod(j, NT)
                        dve.wait_ge(q["tok_put"], n + 1)
                        if j == 0 and u >= 2:
                            dve.wait_ge(q["mt_put"], u - 1)
                        nc.vector.tensor_reduce(mx[:, u % 2, t, g, 0, :],
                                                tok[n % 2][:, 0:KG].rearrange("p (j h) -> p h j", h=HG), AX.X, ALU.max).then_inc(q["tok_maxed"], 1)
                    if job == "q":
                        dve.wait_ge(q["q_hi"], u + 1)
                        if u >= 2:
                            for g in range(G):
                                dve.wait_ge(stack_q[u % 2][g], STQ * (u // 2))
                        nc.vector.scalar_tensor_tensor(qlo[:, u % 2, :], m1[:, :], bq[:, L:L + 1], qhi[:, u % 2, :].bitcast(F32),
                                                       ALU.add, ALU.subtract).then_inc(q["q_lo"], 1)
                    if job == "on":
                        dve.wait_ge(q["on_put"], u + 1)
                        link(nc.vector.reciprocal(rden[:, :, :], m1[:, :].rearrange("p (t h d) -> p t h d", t=NT, h=H)[:, :, :, 0]))
                        if u >= 1:
                            dve.wait_ge(q["ot_put"], u)
                        nc.vector.tensor_tensor(on[:, :, :].rearrange("p t (h d) -> p (t h) d", h=H), m0[:, :].rearrange("p (n d) -> p n d", d=HD),
                                                rden[:, :, :].rearrange("p t h -> p (t h)").unsqueeze(2).broadcast_to([128, NT * H, HD]),
                                                ALU.mult).then_inc(q["o_normed"], 1)
                    if job == "wo":
                        dve.wait_ge(q["att_put"], u + 1)
                        if L == 0:
                            dve.wait_ge(q["xb_set"], NT * (b + 1))
                        nc.vector.tensor_tensor(x[:, NT * b:NT * b + NT, :], m1[:, :].rearrange("p (t d) -> p t d", t=NT),
                                                x[:, NT * b:NT * b + NT, :], ALU.add).then_inc(q["x_attended"], 1)
                        dve.wait_ge(q["x_attended"], u + 1)
                        ln_stats(B * (2 * L + 1) + b)
                    if job == "ln":
                        n = B * (2 * L + 1) + b
                        ln_apply(n)
                        if L == 0:
                            dve.wait_ge(q["xn_ready"], n + 1)
                            nc.vector.tensor_reduce(axb[:, 0, b:b + 1], xn[:, NT * b:NT * b + NT, :], AX.XY, ALU.max, apply_absolute_value=True
                                                    ).then_inc(q["ax_ready"], 1)
                    if job == "max":
                        dve.wait_ge(q["tok_maxed"], 16 * (u + 1))
                        nc.vector.tensor_copy(mx[:, u % 2, :, :, 1, :].rearrange("p t g h -> p (t g) h"),
                                              mx[:, u % 2, :, :, 0, :].rearrange("p t g h -> p (t g) h")).then_inc(q["mx_doubled"], 1)
                        dve.wait_ge(q["mt_hi"], u + 1)
                        if u >= 2:
                            for g in range(G):
                                dve.wait_ge(stack_m[u % 2][g], STM * (u // 2))
                        nc.vector.scalar_tensor_tensor(mthl[:, u % 2, :], mthi[:, :].bitcast(F32), mpart, m0[0:2 * H, :],
                                                       ALU.mult, ALU.add).then_inc(q["mt_split"], 1)
                    if job == "lnstat":
                        dve.wait_ge(x_in[b], 16)
                        ln_stats(b)
                    if job == "lnx0":
                        ln_apply(b)
                        if b == 0:
                            key_split(0)
                    if job == "vr0":
                        v_blocks(0, b)
                    if job == "round":
                        (weight_scales, weights_rounded, extra_mask)[b]()
                    if job == "kt":
                        clip_scales()
                        key_split(1)
                    if job == "vr":
                        v_blocks(1, b)
                    if job == "down":
                        dve.wait_ge(q["d_put"], b + 1)
                        link(nc.vector.tensor_tensor(dtmp[:, b % 2, :].rearrange("p (t d) -> p t d", t=NT),
                                                     acc[b % 2][:, :].rearrange("p (t d) -> p t d", t=NT),
                                                     sdrow[:, :].unsqueeze(1).broadcast_to([128, NT, D]), ALU.mult))
                        v = x[:, NT * b:NT * b + NT, :]
                        nc.vector.tensor_tensor(v, v, dtmp[:, b % 2, :].rearrange("p (t d) -> p t d", t=NT), ALU.add).then_inc(q["x_ffn"], 1)
                        dve.wait_ge(q["x_ffn"], b + 1)
                        ln_stats(2 * B + b)
                    if job == "lnx":
                        ln_apply(2 * B + b)
                    if job == "hround":
                        hidden_rounded(b)
                    if job == "gset":
                        dve.wait_ge(q["gate_in"], 80)
                        link(nc.vector.tensor_copy(gwh, gwf[:, :]))
                        nc.vector.tensor_tensor(gwl, gwf[:, :], gwh.bitcast(F32), ALU.subtract)
                        nc.vector.tensor_reduce(b2s[:, :], b2[:, :], AX.X, ALU.add).then_inc(q["b2_summed"], 1)
                    if job == "x1":
                        x_lo(b)
                    if job == "experts":
                        expert_step(b)

            def hidden_rounded(b):
                v = h0[:, b, :, :]
                link(nc.vector.tensor_scalar(v, v, rqs[:, 1:2], QMAX, ALU.mult, ALU.min))
                nc.vector.tensor_scalar(v, v, -QMAX - 1.0, MAGIC, ALU.max, ALU.add).then_inc(q["hq_f"], 1)
                if b == 0:
                    dve.wait_ge(q["wqT_copied"], 4)
                    link(nc.vector.tensor_scalar(sdrow[:, :], sdrow[:, :], qs[:, 1:2], None, ALU.mult))

            def x_lo(b):
                dve.wait_ge(q["x1_hi"], b + 1)
                if b >= 2:
                    dve.wait_ge(q["w1_put"], NH * (b - 1))
                else:
                    for g in range(G):
                        dve.wait_ge(stack_q[b % 2][g], STQ * B)
                nc.vector.tensor_tensor(xl1[:, b % 2, :], m0[:, :], xh1[:, b % 2, :].bitcast(F32), ALU.subtract).then_inc(q["x1_lo"], 1)

            def bc(ap):
                return ap.unsqueeze(2).broadcast_to([128, NT, E])

            def gate_a(b):
                dve.wait_ge(q["lg_put"], b + 1)
                if b >= 1:
                    dve.wait_ge(q["lg_e"], b)
                both = m1[:, 0:2 * NT * E].rearrange("p (t s e) -> p t s e", t=NT, s=2)
                link(nc.vector.tensor_tensor(lg[:, :, :], both[:, :, 0, :], gb[:, :].unsqueeze(1).broadcast_to([128, NT, E]), ALU.add))
                link(nc.vector.tensor_tensor(lg[:, :, :], both[:, :, 1, :], lg[:, :, :], ALU.add))
                link(nc.vector.tensor_tensor(lq[:, :, :], lg[:, :, :], lg[:, :, :], ALU.mult))
                nc.vector.tensor_reduce(s4[:, 0, :], lq[:, :, :], AX.X, ALU.add).then_inc(q["lg_ms"], 1)

            def gate_b(b):
                dve.wait_ge(q["lg_r"], b + 1)
                link(nc.vector.tensor_tensor(lg[:, :, :], lg[:, :, :], bc(s4[:, 2, :]), ALU.mult))
                link(nc.vector.tensor_tensor(lg[:, :, :], lg[:, :, :], rw[:, :].unsqueeze(1).broadcast_to([128, NT, E]), ALU.mult))
                link(nc.vector.tensor_scalar(lg[:, :, :], lg[:, :, :], 2.0, None, ALU.mult))
                link(nc.vector.tensor_reduce(s4[:, 3, :], lg[:, :, :], AX.X, ALU.max))
                nc.vector.tensor_tensor(lg[:, :, :], lg[:, :, :], bc(s4[:, 3, :]), ALU.subtract).then_inc(q["lg_d"], 1)

            def gate_c(b):
                dve.wait_ge(q["lg_e"], b + 1)
                link(nc.vector.tensor_reduce(s4[:, 4, :], lq[:, :, :], AX.X, ALU.add))
                link(nc.vector.reciprocal(s4[:, 4, :], s4[:, 4, :]))
                link(nc.vector.tensor_scalar(s4[:, 3, :], s4[:, 4, :], 1e-6, None, ALU.add))
                link(nc.vector.reciprocal(s4[:, 3, :], s4[:, 3, :]))
                link(nc.vector.tensor_tensor(ng[:, b % 2, :], s4[:, 4, :], s4[:, 3, :], ALU.mult))

            def expert_step(n):
                if n < NH * B:
                    dve.wait_ge(q["gelu_ready"], n + 1)
                    if n >= HR:
                        dve.wait_ge(q["w2_done"], n - HR + 1)
                    nc.vector.tensor_copy(hh[:, n % HR, :], hf[:, n % HR, :]).then_inc(q["h_split"], 1)
                    dve.wait_ge(q["h_split"], 2 * n + 1)
                    nc.vector.tensor_tensor(hl[:, n % HR, :], hf[:, n % HR, :], hh[:, n % HR, :].bitcast(F32), ALU.subtract).then_inc(q["h_split"], 1)
                b = n // NH
                if n % NH == 8 and 2 <= b + 1 < B:
                    x_lo(b + 1)
                if n == FIRST_A:
                    gate_a(0)
                if n == FIRST_B:
                    gate_b(0)
                if n == FIRST_C:
                    gate_c(0)
                if n % NH == AT_A and b + 1 < B:
                    gate_a(b + 1)
                if n % NH == AT_B and b + 1 < B:
                    gate_b(b + 1)
                if n % NH == AT_C and 1 <= b < B:
                    gate_c(b)
                if n % NH == AT_Y and b >= 1:
                    v = b - 1
                    dve.wait_ge(q["yT_put"], v + 1)
                    for t in range(NT):
                        ins = nc.vector.scalar_tensor_tensor(xn[:, NT * v + t, :], m1[:, 128 * t:128 * t + 128],
                                                             ng[:, v % 2, t:t + 1], x[:, NT * v + t, :], ALU.mult, ALU.add)
                    ins.then_inc(q["y_done"], 1)

            def whole_max(j):
                dve.wait_ge(q["const_set"], 5)
                dve.wait_ge(q["ax_ready"], B)
                nc.vector.tensor_reduce(axm[:, j:j + 1], axb[:, j, :], AX.X, ALU.max).then_inc(q["part_max"], 1)
                dve.wait_ge(q["row_put"], j + 1)
                nc.vector.tensor_reduce(gm1[0:1, j:j + 1], m1[0:1, 0:128], AX.X, ALU.max).then_inc(q["row_max"], 1)
                dve.wait_ge(q["bc_put"], j + 1)
                link(nc.vector.tensor_scalar(qs[:, j:j + 1], m1[:, 256:257], csc[:, j:j + 1], None, ALU.mult))
                nc.vector.reciprocal(rqs[:, j:j + 1], qs[:, j:j + 1]).then_inc(q["rq_ready"], 1)
                dve.wait_ge(q["rq_ready"], j + 1)

            attention(0)
            whole_max(0)

            def x_rounded(b):
                v = xn[:, NT * b:NT * b + NT, :]
                dve.wait_ge(q["nt_copied"], b + 1)
                link(nc.vector.tensor_scalar(v, v, rqs[:, 0:1], QMAX, ALU.mult, ALU.min))
                nc.vector.tensor_scalar(v, v, -QMAX - 1.0, MAGIC, ALU.max, ALU.add).then_inc(q["xq_ready"], 1)

            x_rounded(0)
            for j in range(2):
                nc.vector.tensor_scalar(gus[:, 3 * j:3 * j + 2], wmx[:, 3 * j:3 * j + 2], qs[:, 0:1], None, ALU.mult)
                ins = nc.vector.tensor_scalar(gus[0:IT[2], 3 * j + 2:3 * j + 3], wmx[0:IT[2], 3 * j + 2:3 * j + 3], qs[0:IT[2], 0:1], None, ALU.mult)
            ins.then_inc(q["gus_ready"], 1)
            x_rounded(1)
            for n in range(3 * B):
                b, i3 = divmod(n, 3)
                w = IT[i3]
                dve.wait_ge(q["silu_ready"], n + 1)
                dve.wait_ge(q["u_put"], n + 1)
                nc.vector.scalar_tensor_tensor(h0[0:w, b, i3, :], up_bank[n % 4][0:w, :], gus[0:w, 3 + i3:4 + i3],
                                               sg[0:w, n % 4, :], ALU.mult, ALU.mult).then_inc(q["h_ready"], 1)
                if i3 == 2:
                    dve.wait_ge(q["h_ready"], n + 1)
                    dve.wait_ge(q["h_cleared"], 1)
                    link(nc.vector.tensor_reduce(axb[:, 1, b:b + 1], h0[:, b, :, :], AX.XY, ALU.max, apply_absolute_value=True))
            whole_max(1)
            attention(1)
            for n in range(NH, NH * B + AT_Y + 1):
                expert_step(n)

        @block.tensor
        def _(pe):
            mm = nc.tensor.matmul

            def keys(L):
                if L == 0:
                    pe.wait_ge(q["ctx_in"], 16)
                    pe.wait_ge(q["wkv_in"], 16)
                else:
                    pe.wait_ge(q["wqT_copied"], 3)
                mm((key[0], tok[0])[L][:, 0:B * MP], wk[:, L, :], ctxt[:, :], start=True, stop=True).then_inc(q["kt_put"], 1)

            def values(L, b):
                if L == 0:
                    pe.wait_ge(q["ctxr_ready"], 1)
                    if b >= 2:
                        pe.wait_ge(q["v_set"], b - 1)
                if L == 1:
                    if b < 2:
                        pe.wait_ge(q["k_split"], 2)
                        pe.wait_ge(q["wqT_copied"], 4)
                    else:
                        pe.wait_ge(q["v_set"], B + b - 1)
                bank = (acc, tok)[L][b % 2]
                for c in range(NC):
                    lo = b * MP + c * JC
                    ins = mm(bank[0:PR, D * c:D * c + D], ctxr[:, lo:lo + JC, :].rearrange("p j h -> p (j h)"), wv[:, L, :], start=True, stop=True)
                ins.then_inc(q["vr_put"], 1)

            def weights_transposed(j):
                if j == 0:
                    pe.wait_ge(q["wq_rounded"], 1)
                    pe.wait_ge(q["tok_maxed"], 16 * B)
                if j >= 2:
                    pe.wait_ge(q["wqT_copied"], j - 1)
                if j < 2:
                    w = (wg0, wu0)[j]
                    for t in range(3):
                        ins = nc.tensor.transpose(tok[j][:, 128 * t:128 * t + IT[t]], w[0:IT[t], t, :], ident[0:IT[t], 0:IT[t]])
                    ins.then_inc(q["wqT_put"], 1)
                if j == 2:
                    for t in range(3):
                        ins = nc.tensor.transpose(tok[0][0:IT[t], 128 * t:128 * t + 128], wd0[:, 128 * t:128 * t + IT[t]], ident[:, :])
                    ins.then_inc(q["wqT_put"], 1)
                if j == 3:
                    pe.wait_ge(q["sd_diag"], 1)
                    pe.wait_ge(q["const_set"], 5)
                    mm(tok[1][:, 0:D], ones[:, :], diag[:, :], start=True, stop=True).then_inc(q["sd_put"], 1)

            def down(b):
                pe.wait_ge(q["hq_ready"], b + 1)
                if b >= 2:
                    pe.wait_ge(q["x_ffn"], b - 1)
                for t in range(NT):
                    for i3 in range(3):
                        w = IT[i3]
                        ins = mm(acc[b % 2][:, 128 * t:128 * t + 128], hq[0:w, b, i3, 128 * t:128 * t + 128], wdT[0:w, i3, :],
                                 start=(i3 == 0), stop=(i3 == 2))
                ins.then_inc(q["d_put"], 1)

            def attention(L):
                for job, b, j in order(L):
                    u = B * L + b
                    if job == "xt":
                        pe.wait_ge(q["xn_ready"], 2 * B * L + b + 1)
                        m0_free()
                        if u == 0:
                            pe.wait_ge(q["consts_in"], 16)
                        for t in range(NT):
                            ins = nc.tensor.transpose(m0[:, 128 * t:128 * t + 128], xn[:, NT * b + t, :], ident[:, :])
                        ins.then_inc(q["xt_put"], 1)
                        n_xt[0] += 1
                    if job == "tok":
                        s, n = u % 3, 16 * u + j
                        g, t = divmod(j, NT)
                        if t == 0:
                            pe.wait_ge(stack_q[u % 2][g], STQ * (u // 2 + 1))
                            pe.wait_ge(kst_in[g], 48 * (L + 1))
                            if j == 0:
                                pe.wait_ge(q["krow_set"], u + 1)
                                pe.wait_ge(q["const_set"], 5)
                        if n >= 2:
                            pe.wait_ge(q["tok_maxed"], n - 1)
                        mm(tok[n % 2][:, 0:KG], qst[0:MASKROW + 1, s, g, 128 * t:128 * t + 128], kst[0:MASKROW + 1, b, g, :],
                           start=True, stop=True).then_inc(q["tok_put"], 1)
                    if job == "key":
                        n = 12 * u + j
                        c, g = divmod(j, G)
                        if c == 0:
                            pe.wait_ge(stack_m[u % 2][g], STM * (u // 2 + 1))
                        if n >= 2:
                            pe.wait_ge(q["p_ready"], n - 1)
                        mm(key[n % 2][0:PR, :], kst[0:KROWS, b, g, PR * c:PR * c + PR], qst[0:KROWS, u % 3, g, :],
                           start=True, stop=True).then_inc(q["key_put"], 1)
                    if job == "pv":
                        probs_v(L, b, j // 2, j % 2)
                    if job == "q":
                        pe.wait_ge(q["xt_copied"], u + 1)
                        pe.wait_ge(q["wqo_in"], 16)
                        m1_free()
                        mm(m1[:, :], wq[:, L, :], xt[:, u % 2, :], start=True, stop=True).then_inc(q["q_put"], 1)
                        n_q[0] += 1
                    if job == "on":
                        pe.wait_ge(q["o_copied"], u + 1)
                        m0_free()
                        for t in range(NT):
                            nc.tensor.transpose(m0[:, 128 * t:128 * t + 128], ov[:, 128 * t:128 * t + 128], ident[:, :])
                        m1_free()
                        for t in range(NT):
                            ins = nc.tensor.transpose(m1[:, 128 * t:128 * t + 128], od[:, 128 * t:128 * t + 128], ident[:, :])
                        ins.then_inc(q["on_put"], 1)
                        n_on[0] += 1
                    if job == "ot":
                        m0_free()
                        for t in range(NT):
                            ins = nc.tensor.transpose(m0[:, 128 * t:128 * t + 128], on[:, t, :], ident[:, :])
                        ins.then_inc(q["ot_put"], 1)
                        n_ot[0] += 1
                    if job == "wo":
                        pe.wait_ge(q["ot_copied"], u + 1)
                        m1_free()
                        for t in range(NT):
                            ins = mm(m1[:, 128 * t:128 * t + 128], ot[:, 128 * t:128 * t + 128], wo[:, L, :], start=True, stop=True)
                        ins.then_inc(q["att_put"], 1)
                        n_wo[0] += 1
                    if job == "max":
                        pe.wait_ge(q["mx_doubled"], u + 1)
                        m0_free()
                        for t in range(NT):
                            both = mx[:, u % 2, t].rearrange("p g s h -> p (g s h)")
                            ins = nc.tensor.transpose(m0[0:2 * H, 128 * t:128 * t + 128], both, ident[:, :])
                        ins.then_inc(q["mt_put"], 1)
                        n_mt[0] += 1
                    if job == "wqt":
                        weights_transposed(b)
                    if job == "kt":
                        keys(1)
                    if job == "vr0":
                        values(0, b)
                    if job == "vr":
                        values(1, b)
                    if job == "down":
                        down(b)
                    if job == "nt":
                        pe.wait_ge(q["xn_ready"], B + b + 1)
                        m0_free()
                        for t in range(NT):
                            ins = nc.tensor.transpose(m0[:, 128 * t:128 * t + 128], xn[:, NT * b + t, :], ident[:, :])
                        ins.then_inc(q["nt_put"], 1)
                        n_nt[0] += 1
                    if job == "x1":
                        x_transposed(b)
                    if job == "experts":
                        expert_step(b)

            def x_transposed(b):
                pe.wait_ge(q["xn_ready"], 3 * B + b + 1)
                m0_free()
                for t in range(NT):
                    ins = nc.tensor.transpose(m0[:, 128 * t:128 * t + 128], xn[:, NT * b + t, :], ident[:, :])
                ins.then_inc(q["xt1_put"], 1)
                n_x1[0] += 1

            def logits(b):
                pe.wait_ge(q["x1_lo"], b + 1)
                pe.wait_ge(q["b2_summed"], 1)
                m1_free()
                for t in range(NT):
                    tt = slice(128 * t, 128 * t + 128)
                    for j, xs in enumerate((xh1, xl1)):
                        ins = mm(m1[:, 2 * E * t:2 * E * t + 2 * E], xs[:, b % 2, tt], gwhl[:, :, :].rearrange("p s e -> p (s e)"),
                                 start=(j == 0), stop=(j == 1))
                ins.then_inc(q["lg_put"], 1)
                n_lg[0] += 1

            def expert_step(n):
                b, j = divmod(n, NH)
                if n < NH * B:
                    w = slice(128 * j, 128 * j + 128)
                    bank = (tok + key)[n % 4]
                    if n == 0:
                        pe.wait_ge(q["w1_split"], 1)
                        pe.wait_ge(q["tok_maxed"], 32 * B)
                        pe.wait_ge(q["p_ready"], 24 * B)
                    if n >= 4:
                        pe.wait_ge(q["gelu_ready"], n - 3)
                    if j == 0:
                        pe.wait_ge(q["x1_lo"], b + 1)
                    mm(bank[:, :], w1l[:, w], xh1[:, b % 2, :], start=True, stop=False)
                    mm(bank[:, :], w1h[:, w], xl1[:, b % 2, :], start=False, stop=False)
                    mm(bank[:, :], w1h[:, w], xh1[:, b % 2, :], start=False, stop=True).then_inc(q["w1_put"], 1)
                m = n - HLAG
                if 0 <= m < NH * B:
                    bm, jm = divmod(m, NH)
                    w = slice(128 * jm, 128 * jm + 128)
                    pe.wait_ge(q["h_split"], 2 * m + 2)
                    if m == 0:
                        pe.wait_ge(q["w2_split"], 1)
                        pe.wait_ge(q["o_copied"], 2 * B)
                    if jm == 0 and bm >= 2:
                        pe.wait_ge(q["yt_copied"], bm - 1)
                    mm(acc[bm % 2][:, :], w2l[:, w], hh[:, m % HR, :], start=(jm == 0), stop=False)
                    mm(acc[bm % 2][:, :], w2h[:, w], hl[:, m % HR, :], start=False, stop=False)
                    mm(acc[bm % 2][:, :], w2h[:, w], hh[:, m % HR, :], start=False, stop=(jm == NH - 1)).then_inc(q["w2_done"], 1)
                if j == 8 and 2 <= b + 1 < B:
                    x_transposed(b + 1)
                if j == AT_YT and b >= 1:
                    pe.wait_ge(q["yt_copied"], b)
                    m1_free()
                    for t in range(NT):
                        ins = nc.tensor.transpose(m1[:, 128 * t:128 * t + 128], yt[:, 128 * t:128 * t + 128], ident[:, :])
                    ins.then_inc(q["yT_put"], 1)
                    n_y[0] += 1
                if n == FIRST_LOG:
                    logits(0)
                if j == AT_LOG and b + 1 < B:
                    logits(b + 1)

            def probs_v(L, b, c, den):
                u = B * L + b
                if den == 0:
                    pe.wait_ge(q["p_ready"], 12 * u + G * (c + 1))
                    if c == 0 and u >= 1:
                        pe.wait_ge(q["o_copied"], u)
                    if c == 0:
                        pe.wait_ge(q["v_set"], B * (L + 1))
                    if c == 0 and u == B:
                        pe.wait_ge(q["x_ffn"], B)
                for g in range(G):
                    w = vmask if den else vbd[:, L, b, c, 32 * g:32 * g + 32]
                    ins = mm(acc[den][32 * g:32 * g + 32, :], w, p[:, G * c + g, :], start=(c == 0), stop=(c == NC - 1))
                if den:
                    ins.then_inc(q["pv_put"], 1)

            n_on, n_ot, n_xt, n_mt, n_wo, n_q, n_nt, n_x1, n_lg, n_y = ([0] for _ in range(10))

            def m0_free():
                for count, name in ((n_on, "o_normed"), (n_ot, "ot_copied"), (n_xt, "xt_copied"), (n_mt, "mt_split"),
                                    (n_nt, "nt_copied"), (n_x1, "x1_lo")):
                    if count[0]:
                        pe.wait_ge(q[name], count[0])

            def m1_free():
                for count, name in ((n_on, "o_normed"), (n_wo, "x_attended"), (n_q, "q_lo"), (n_lg, "lg_ms"), (n_y, "y_done")):
                    if count[0]:
                        pe.wait_ge(q[name], count[0])

            def whole_max(j):
                pe.wait_ge(q["part_max"], j + 1)
                mm(m1[0:1, 0:128], axm[:, j:j + 1], ident[:, :], start=True, stop=True).then_inc(q["row_put"], 1)
                pe.wait_ge(q["row_max"], j + 1)
                mm(m1[:, 256:257], ones[0:1, :], gm1[0:1, j:j + 1], start=True, stop=True).then_inc(q["bc_put"], 1)

            keys(0)
            attention(0)
            whole_max(0)
            for n in range(3 * B):
                b, i3 = divmod(n, 3)
                w, lo = IT[i3], 128 * i3
                pe.wait_ge(q["xqt_copied"], b + 1)
                if n >= 4:
                    pe.wait_ge(q["silu_ready"], n - 3)
                mm(gate_bank[n % 4][0:w, :], wgT[:, lo:lo + w], xqt[:, b, :], start=True, stop=True).then_inc(q["g_put"], 1)
                if n == 2:
                    m0_free()
                if n >= 4:
                    pe.wait_ge(q["h_ready"], n - 3)
                mm(up_bank[n % 4][0:w, :], wuT[:, lo:lo + w], xqt[:, b, :], start=True, stop=True).then_inc(q["u_put"], 1)
            whole_max(1)
            attention(1)
            for n in range(NH, NH * B + AT_YT + 1):
                expert_step(n)


def shape_constants():
    cst = np.zeros((128, 133 + HG * HD), np.float32)
    cst[:, 0:128] = np.eye(128)
    d = np.arange(128)
    cst[:, 128:132] = (d // HD % HG)[:, None] == np.arange(HG)[None]
    cst[0:2 * H, 132] = -(np.arange(2 * H) // HG % 2)
    cst[0:PR, 133:] = (np.arange(PR) % HG)[:, None] == (np.arange(HG * HD) // HD)[None]
    rows = np.zeros((KROWS - 96, B, MP, HG), np.float32)
    rows[0, :, M:, :] = 1.5 * NEG
    for h in range(HG):
        rows[MHI - 96 + h, :, :, h] = -1.0
        rows[MLO - 96 + h, :, :, h] = -1.0
    return cst, rows.reshape(KROWS - 96, B * KG)


def kernel(**inputs):
    import concourse.bacc as _bacc
    from concourse.bass_utils import run_bass_kernel_spmd as _run

    v = {k: np.asarray(w) for k, w in inputs.items()}
    cst, rows = shape_constants()
    kv = v["L0_xattn_Wkv"].reshape(H, 2, HD, C)
    bkv = v["L0_xattn_bkv"].reshape(H, 2, HD)
    zero = np.zeros((1, D), np.float32)
    ctx = np.zeros((C + 1, B, MP), np.float32)
    ctx[C] = 1.0
    ctx[0:C, :, 0:M] = v["ctx_768"].transpose(2, 0, 1)
    arrays = {
        "x": v["x"],
        "cst": cst, "krows": rows,
        "ctxT": ctx.reshape(C + 1, B * MP),
        "mask": v["mask_BxS2_bf1"].view(np.uint8),
        "wkv": np.stack([np.concatenate([kv[:, 0].reshape(D, C).T, bkv[:, 0].reshape(1, D)]),
                         np.concatenate([v["L1_xattn_Wk"], zero]),
                         np.concatenate([kv[:, 1].reshape(D, C).T, bkv[:, 1].reshape(1, D)]),
                         np.concatenate([v["L1_xattn_Wv"], zero])], 1),
        "wqo": np.stack([v["L0_xattn_Wq"].T, v["L1_xattn_Wq"], v["L0_xattn_Wo"].T, v["L1_xattn_Wo"]], 1),
        "bq": v["L0_xattn_bq"].reshape(D, 1),
        "bo": v["L0_xattn_bo"],
        "clip": np.concatenate([v["L0_ffn_clip_x"], v["L0_ffn_clip_down"]]),
        "w_gate": v["L0_ffn_w_gate"], "w_up": v["L0_ffn_w_up"], "w_down": v["L0_ffn_w_down"],
        "gate_wT": v["L1_ffn_gate_w"].T, "gate_b": v["L1_ffn_gate_b"], "rms_w": v["L1_ffn_rms_w"],
        "w1": v["L1_ffn_w1"], "b1": v["L1_ffn_b1"].reshape(NH, 128).T,
        "w2": v["L1_ffn_w2"], "b2": v["L1_ffn_b2"].T,
    }
    nc = _bacc.Bacc("TRN2", target_bir_lowering=False, num_devices=1)
    feeds, aps = {}, {}
    for name, w in arrays.items():
        w = np.ascontiguousarray(w)
        feeds["in_" + name] = w
        aps[name] = nc.dram_tensor("in_" + name, w.shape, mybir.dt.from_np(w.dtype), kind="ExternalInput").ap()
    out = nc.dram_tensor("out_0", (B, S, D), F32, kind="ExternalOutput").ap()
    build(nc, aps, out)
    r = _run(nc, [feeds], core_ids=[0])
    return r.results[0]["out_0"]
```
